# Optimizing a Trainium2 kernel written in Bass

```python
import numpy as np
import jax
import jax.numpy as jnp

def _softmax(x, axis=-1):
    return jax.nn.softmax(x, axis=axis)

def _gelu(x):
    return jax.nn.gelu(x, approximate=True)

def _silu(x):
    return jax.nn.silu(x)

def _sigmoid(x):
    return jax.nn.sigmoid(x)

def _layernorm(x, axis=-1, eps=1e-05):
    m = jnp.mean(x, axis=axis, keepdims=True)
    v = jnp.var(x, axis=axis, keepdims=True)
    return (x - m) / jnp.sqrt(v + eps)

def _scatter_add(tgt, idx, src, axis=0):
    return tgt.at[idx].add(src)

def _segment_sum(src, seg, n):
    return jax.ops.segment_sum(src, seg, n)
kernel_name = 'mk_conv_preact_d2_conv_nchw256_r4_45886f'

def setup_inputs(seed: int=0):
    np.random.seed(seed)
    _w = jnp.asarray

    def _rec_inputs():
        import jax
        import jax.numpy as jnp
        _gk = jax.random.key(seed)
        x = 7.22e-05 + 1 * jax.random.normal(jax.random.fold_in(_gk, 1), (8, 64, 16, 16), jnp.float32)
        return x
    x = _rec_inputs()

    def _L0_conv_setup():
        import jax, jax.numpy as jnp
        from jax import lax
        import numpy as np
        NUM_HEADS = 8
        KW = 3

        def _avgpool3(x):
            s = lax.reduce_window(x, 0.0, lax.add, (1, 1, KW, KW), (1, 1, 1, 1), ((0, 0), (0, 0), (1, 1), (1, 1)))
            return s / (KW * KW)

        def _unfold3(y):
            B, h, w, C = y.shape
            yp = jnp.pad(y, ((0, 0), (1, 1), (1, 1), (0, 0)))
            return jnp.stack([yp[:, i:i + h, j:j + w, :] for i in range(KW) for j in range(KW)], axis=3)
        key = jax.random.key(seed)
        ks = jax.random.split(key, 9)
        B, C, H, W = (8, 64, 16, 16)
        sd = 0.02
        return {'x': jax.random.normal(ks[0], (B, C, H, W), jnp.float32), 'W_qkv': jax.random.normal(ks[1], (4 * C, C), jnp.float32) * sd, 'b_qkv': jnp.zeros((4 * C,), jnp.float32), 'W1': jax.random.normal(ks[2], (C // 2, C), jnp.float32) * sd, 'b1': jnp.zeros((C // 2,), jnp.float32), 'W2': jax.random.normal(ks[3], (C, C // 2), jnp.float32) * sd, 'b2': jnp.zeros((C,), jnp.float32), 'Wp': jax.random.normal(ks[4], (C, C), jnp.float32) * sd, 'bp': jnp.zeros((C,), jnp.float32)}
    _L0_conv_all = _L0_conv_setup()
    _L0_conv_in = {k: v for k, v in _L0_conv_all.items() if k in ('W_qkv', 'b_qkv', 'W1', 'b1', 'W2', 'b2', 'Wp', 'bp')}
    del _L0_conv_all

    def _L1_conv_setup():
        import jax, jax.numpy as jnp
        import numpy as np
        DG, K, PAD = (4, 3, 1)
        K2 = K * K

        def _mdcn(x, offset, mask, weight):
            B, C, H, W = x.shape
            Cg = C // DG
            off = offset.reshape(B, DG, K2, 2, H, W)
            dy, dx = (off[:, :, :, 0], off[:, :, :, 1])
            m = mask.reshape(B, DG, K2, H, W)
            ki = jnp.repeat(jnp.arange(K), K)
            kj = jnp.tile(jnp.arange(K), K)
            hh = jnp.arange(H, dtype=x.dtype)
            ww = jnp.arange(W, dtype=x.dtype)
            py = hh[None, None, None, :, None] - PAD + ki[None, None, :, None, None] + dy
            px = ww[None, None, None, None, :] - PAD + kj[None, None, :, None, None] + dx
            y0 = jnp.floor(py)
            x0 = jnp.floor(px)
            wy = py - y0
            wx = px - x0
            y0i = y0.astype(jnp.int32)
            x0i = x0.astype(jnp.int32)
            xf = x.reshape(B, DG, Cg, H * W)

            def gather(yi, xi):
                valid = ((yi >= 0) & (yi < H) & (xi >= 0) & (xi < W)).astype(x.dtype)
                idx = jnp.clip(yi, 0, H - 1) * W + jnp.clip(xi, 0, W - 1)
                g = jnp.take_along_axis(xf, idx.reshape(B, DG, 1, K2 * H * W), axis=3)
                return g.reshape(B, DG, Cg, K2, H, W) * valid[:, :, None]
            v = gather(y0i, x0i) * ((1 - wy) * (1 - wx))[:, :, None] + gather(y0i, x0i + 1) * ((1 - wy) * wx)[:, :, None] + gather(y0i + 1, x0i) * (wy * (1 - wx))[:, :, None] + gather(y0i + 1, x0i + 1) * (wy * wx)[:, :, None]
            v = v * m[:, :, None]
            wr = weight.reshape(-1, DG, Cg, K2)
            return jnp.einsum('ogck,bgckhw->bohw', wr, v)
        key = jax.random.key(seed)
        k1, k2, k3, k4 = jax.random.split(key, 4)
        B, C, H, W, O = (2, 64, 50, 50, 64)
        x = jax.random.normal(k1, (B, C, H, W), jnp.float32)
        w_om = jax.random.normal(k2, (DG * 3 * K2, C, K, K), jnp.float32) * 0.01
        b_om = jax.random.normal(k3, (DG * 3 * K2,), jnp.float32) * 0.1
        w_dcn = jax.random.normal(k4, (O, C, K, K), jnp.float32) * (1.0 / np.sqrt(C * K2))
        return {'x': x, 'w_om': w_om, 'b_om': b_om, 'w_dcn': w_dcn}
    _L1_conv_all = _L1_conv_setup()
    _L1_conv_in = {k: v for k, v in _L1_conv_all.items() if k in ('w_om', 'b_om', 'w_dcn')}
    del _L1_conv_all
    return {'x': x, 'L0_conv_W_qkv': _L0_conv_in['W_qkv'], 'L0_conv_b_qkv': _L0_conv_in['b_qkv'], 'L0_conv_W1': _L0_conv_in['W1'], 'L0_conv_b1': _L0_conv_in['b1'], 'L0_conv_W2': _L0_conv_in['W2'], 'L0_conv_b2': _L0_conv_in['b2'], 'L0_conv_Wp': _L0_conv_in['Wp'], 'L0_conv_bp': _L0_conv_in['bp'], 'L1_conv_w_om': _L1_conv_in['w_om'], 'L1_conv_b_om': _L1_conv_in['b_om'], 'L1_conv_w_dcn': _L1_conv_in['w_dcn']}

def reference(x, L0_conv_W_qkv, L0_conv_b_qkv, L0_conv_W1, L0_conv_b1, L0_conv_W2, L0_conv_b2, L0_conv_Wp, L0_conv_bp, L1_conv_w_om, L1_conv_b_om, L1_conv_w_dcn):
    import jax
    import jax.numpy as jnp

    def _L0_conv_ref(x, W_qkv, b_qkv, W1, b1, W2, b2, Wp, bp):
        import jax, jax.numpy as jnp
        from jax import lax
        import numpy as np
        NUM_HEADS = 8
        KW = 3

        def _avgpool3(x):
            s = lax.reduce_window(x, 0.0, lax.add, (1, 1, KW, KW), (1, 1, 1, 1), ((0, 0), (0, 0), (1, 1), (1, 1)))
            return s / (KW * KW)

        def _unfold3(y):
            B, h, w, C = y.shape
            yp = jnp.pad(y, ((0, 0), (1, 1), (1, 1), (0, 0)))
            return jnp.stack([yp[:, i:i + h, j:j + w, :] for i in range(KW) for j in range(KW)], axis=3)
        B, C, H, W = x.shape
        nH = NUM_HEADS
        hd = C // nH
        scale = hd ** (-0.5)
        y = _avgpool3(x).transpose(0, 2, 3, 1)
        qkv = y @ W_qkv.T + b_qkv
        qkv = qkv.reshape(B, H, W, C, 4)
        q, k, v, chans = (qkv[..., 0], qkv[..., 1], qkv[..., 2], qkv[..., 3])
        g = jax.nn.sigmoid(jax.nn.relu(chans @ W1.T + b1) @ W2.T + b2)
        qh = q.reshape(B, H, W, nH, hd)
        kp = _unfold3(k).reshape(B, H, W, KW * KW, nH, hd)
        vp = _unfold3(v).reshape(B, H, W, KW * KW, nH, hd)
        attn = jnp.einsum('bhwnd,bhwknd->bhwnk', qh, kp) * scale
        attn = jax.nn.softmax(attn, axis=-1)
        out = jnp.einsum('bhwnk,bhwknd->bhwnd', attn, vp).reshape(B, H, W, C)
        out = out * g + out
        out = out @ Wp.T + bp
        return out.transpose(0, 3, 1, 2)

    def _L1_conv_ref(x, w_om, b_om, w_dcn):
        import jax, jax.numpy as jnp
        import numpy as np
        DG, K, PAD = (4, 3, 1)
        K2 = K * K

        def _mdcn(x, offset, mask, weight):
            B, C, H, W = x.shape
            Cg = C // DG
            off = offset.reshape(B, DG, K2, 2, H, W)
            dy, dx = (off[:, :, :, 0], off[:, :, :, 1])
            m = mask.reshape(B, DG, K2, H, W)
            ki = jnp.repeat(jnp.arange(K), K)
            kj = jnp.tile(jnp.arange(K), K)
            hh = jnp.arange(H, dtype=x.dtype)
            ww = jnp.arange(W, dtype=x.dtype)
            py = hh[None, None, None, :, None] - PAD + ki[None, None, :, None, None] + dy
            px = ww[None, None, None, None, :] - PAD + kj[None, None, :, None, None] + dx
            y0 = jnp.floor(py)
            x0 = jnp.floor(px)
            wy = py - y0
            wx = px - x0
            y0i = y0.astype(jnp.int32)
            x0i = x0.astype(jnp.int32)
            xf = x.reshape(B, DG, Cg, H * W)

            def gather(yi, xi):
                valid = ((yi >= 0) & (yi < H) & (xi >= 0) & (xi < W)).astype(x.dtype)
                idx = jnp.clip(yi, 0, H - 1) * W + jnp.clip(xi, 0, W - 1)
                g = jnp.take_along_axis(xf, idx.reshape(B, DG, 1, K2 * H * W), axis=3)
                return g.reshape(B, DG, Cg, K2, H, W) * valid[:, :, None]
            v = gather(y0i, x0i) * ((1 - wy) * (1 - wx))[:, :, None] + gather(y0i, x0i + 1) * ((1 - wy) * wx)[:, :, None] + gather(y0i + 1, x0i) * (wy * (1 - wx))[:, :, None] + gather(y0i + 1, x0i + 1) * (wy * wx)[:, :, None]
            v = v * m[:, :, None]
            wr = weight.reshape(-1, DG, Cg, K2)
            return jnp.einsum('ogck,bgckhw->bohw', wr, v)
        om = jax.lax.conv_general_dilated(x, w_om, (1, 1), ((PAD, PAD), (PAD, PAD)), dimension_numbers=('NCHW', 'OIHW', 'NCHW')) + b_om[None, :, None, None]
        o1, o2, mask = jnp.split(om, 3, axis=1)
        offset = jnp.concatenate([o1, o2], axis=1)
        mask = jax.nn.sigmoid(mask)
        return jax.nn.relu(_mdcn(x, offset, mask, w_dcn))

    def _gn(v, G=32, eps=1e-05):
        B_, C_, H_, W_ = v.shape
        g = v.reshape(B_, G, C_ // G, H_, W_)
        m = jnp.mean(g, axis=(2, 3, 4), keepdims=True)
        s = jnp.var(g, axis=(2, 3, 4), keepdims=True)
        return ((g - m) / jnp.sqrt(s + eps)).reshape(v.shape)

    def _ln_c(v, eps=1e-06):
        m = jnp.mean(v, axis=1, keepdims=True)
        s = jnp.var(v, axis=1, keepdims=True)
        return (v - m) / jnp.sqrt(s + eps)

    def _ln_t(v, eps=1e-05):
        m = jnp.mean(v, axis=-1, keepdims=True)
        s = jnp.var(v, axis=-1, keepdims=True)
        return (v - m) / jnp.sqrt(s + eps)

    def _to_tokens(v):
        B_, C_, H_, W_ = v.shape
        return v.reshape(B_, C_, H_ * W_).transpose(0, 2, 1)

    def _from_tokens(t, like):
        B_, C_, H_, W_ = like.shape
        return t.transpose(0, 2, 1).reshape(B_, C_, H_, W_)
    x = x + _L0_conv_ref(_gn(x), L0_conv_W_qkv, L0_conv_b_qkv, L0_conv_W1, L0_conv_b1, L0_conv_W2, L0_conv_b2, L0_conv_Wp, L0_conv_bp)
    x = x + _L1_conv_ref(_gn(x), L1_conv_w_om, L1_conv_b_om, L1_conv_w_dcn)
    return x

_drawn_inputs = setup_inputs


def setup_inputs(seed=0):
    import zlib

    import numpy as np

    out = dict(_drawn_inputs(seed))
    spreads = {'L0_conv_b_qkv': (0.0, 0.301),
     'L0_conv_b1': (0.0, 2.0),
     'L0_conv_b2': (0.0, 2.0),
     'L0_conv_bp': (0.0, 0.1)}
    factors = {'L0_conv_W_qkv': 6.861, 'L0_conv_W1': 64.0, 'L0_conv_W2': 64.0}
    for name, (base, spread) in spreads.items():
        noise = np.random.default_rng([zlib.crc32(name.encode()), seed]).standard_normal(out[name].shape)
        drawn = base * np.exp(spread * noise) if base else spread * noise
        out[name] = jnp.asarray(drawn.astype(out[name].dtype))
    for name, factor in factors.items():
        out[name] = (out[name] * factor).astype(out[name].dtype)
    return out
```

```python
import concourse.bass as bass
from concourse import mybir
from contextlib import ExitStack

B, C, H, W = 8, 64, 16, 16
HW = H * W
HALVES = 2
J = B // HALVES
P = HALVES * C
N = J * HW
ALL = B * HW
TAPS = 9
PH, PW = H + 2, W + 2
HEADS, HD = 8, 8
SCALE = float(HD) ** -0.5
EPS = 1e-5
GC = 2
DG = 4
CG = C // DG
PAIRS = (TAPS + 1) // 2
OM = 3 * DG * TAPS
ND = DG * TAPS
STACK = 3 * ND
STRIP = 4
STRIPS = H // STRIP
WROWS = P // W
REACH = 2
SHIFTS = 5
WINS = 3 * STRIPS
SROWS = (STRIPS - 1) * STRIP + 2 + WROWS
FIRST_ROW = -(1 + REACH) - WROWS * (SHIFTS // 2)
TROWS = WROWS * (SHIFTS - 1) + SROWS
UNITS = PAIRS * DG
AHEAD = 2
UP = UNITS * B + AHEAD
HP = PAIRS * (B + 1)
BANK = 512


def bass_local_attention_then_deformable_conv(nc, x, cf, wom, biases, tables, sel16, rows16, out):
    fp32, bf16, fp16 = mybir.dt.float32, mybir.dt.bfloat16, mybir.dt.float16
    i32, u16 = mybir.dt.int32, mybir.dt.uint16
    ALU = mybir.AluOpType
    ACT = mybir.ActivationFunctionType
    AX = mybir.AxisListType
    CONSTS = [("gnp", P), ("ident", P), ("wfin", PAIRS * C), ("wqkv", 4 * P), ("w1", P), ("w2", P), ("wp", P),
              ("headsum", J * P)]
    SELS = [("sely", PAIRS * P), ("selx", TAPS * P), ("selm", PAIRS * P)]

    with ExitStack() as ctx:
        def sb(name, shape, dt=fp32):
            return ctx.enter_context(nc.sbuf_tensor(name, shape, dt))

        def sem(name):
            return ctx.enter_context(nc.semaphore(name))

        cst = {name: sb(f"c_{name}", [P, n]) for name, n in CONSTS[:3]}
        gnp, ident = cst["gnp"], cst["ident"]
        bias = sb("bias", [P, 8])
        table = sb("table", [P, SHIFTS])
        sel = {name: sb(f"s_{name}", [STACK + 2, n], bf16) for name, n in SELS}
        bcast = sb("bcast", [P, (DG + 2 * DG + J) * P], fp16)
        b2half = sb("b2half", [P, 1])
        minushalf = sb("minushalf", [P, J])
        one = sb("one", [P, 1])
        stat = sb("stat", [P, 4 * J])
        rstd = sb("rstd", [P, J])

        def shared(name, first, then):
            size = max(sum(n for _, n in first), sum(n for _, n in then))
            words, views = sb(name, [P, size]), {}
            for names in (first, then):
                at = 0
                for key, n in names:
                    views[key] = words[:, at:at + n]
                    at += n
            return views

        PAD, XSW = J * PH * PW, 3 * CG
        m = shared("attention_weights", CONSTS[3:], [("vals1", PAIRS * HW)])
        cst.update({name: m[name] for name, _ in CONSTS[3:]})
        vals = [sb("vals0", [P, PAIRS * HW]), m["vals1"]]
        m = shared("womt_hx", [("womt", HALVES * TAPS * OM)], [("hx", 4 * BANK)])
        womt, hx = m["womt"], m["hx"]
        m = shared("x_smp", [("xin", N), ("x2", N)], [("smp", 4 * BANK)])
        xin, x2, smp = m["xin"], m["x2"], m["smp"]
        m = shared("norm_om", [("xc", N), ("sq", N)], [("om", ALL)])
        xc, sq, om = m["xc"], m["sq"], m["om"][0:OM]
        m = shared("img_staged", [("img", PAD)], [("staged", J * SROWS * W)])
        img, staged = m["img"], m["staged"]
        m = shared("prod_maskb", [("prod", TAPS * N)], [("maskb", PAIRS * ALL)])
        prod, maskb = m["prod"], m["maskb"]

        WX, XS = J * WINS * P, WINS * DG * XSW
        arena = sb("arena", [P, WX + J * TROWS * W + 2 * XS])
        at = 0
        views = {}
        for key in ("pooled", "q", "chans", "hidden", "gate", "att"):
            views[key] = arena[:, at:at + N]
            at += N
        pooled, q, chans, hidden, gate, att = (views[k] for k in ("pooled", "q", "chans", "hidden", "gate", "att"))
        rest = arena[0:OM, 0:ALL]
        part = [arena[0:OM, ALL + i * N:ALL + (i + 1) * N].bitcast(bf16) for i in range(3)]
        xT = arena[:, 0:WX + WINS * P]
        at = WX
        for key, n in (("kpad", PAD), ("vpad", PAD), ("hsum", J * PH * W), ("dlog", TAPS * HW), ("lmax", HW),
                       ("den", HW)):
            views[key] = arena[:, at:at + n]
            at += n
        kpad, vpad, hsum, dlog, lmax, den = (views[k] for k in ("kpad", "vpad", "hsum", "dlog", "lmax", "den"))
        tall = arena[:, WX:WX + J * TROWS * W]
        at = WX + J * TROWS * W
        xs = [arena[:, at + i * XS:at + (i + 1) * XS] for i in range(2)]

        stack = {k: sb(f"stack_{k}", [STACK + 2, ALL], bf16) for k in "ymx"}
        amax = sb("amax", [OM, 1])
        far = sb("far", [1, 2])
        choice = sb("choice", [1, 2], i32)
        ybias = sb("ybias", [P, 1])
        distx = sb("distx", [P, BANK])
        disty = sb("disty", [P, HW])
        hatx = sb("hatx", [P, TAPS * HW], fp16)
        prob16 = hatx
        haty = sb("haty", [P, PAIRS * HW], fp16)
        acc = sb("acc", [C, (B + 1) * HW])
        x2seq = sb("x2seq", [C, ALL])

        ps = ctx.enter_context(nc.psum_tensor("ps", [P, 8 * BANK], fp32))

        def bank(i, n=1):
            return ps[:, i * BANK:(i + n) * BANK]

        def images(t, w=HW):
            return t[:, :].rearrange("p (j n) -> p j n", j=J)

        def padded(t):
            return t[:, :].rearrange("p (j r c) -> p j r c", j=J, r=PH)

        def shifted(t, tap):
            return padded(t)[:, :, tap // 3:tap // 3 + H, tap % 3:tap % 3 + W]

        def grid(ap):
            return ap.rearrange("p (j r c) -> p j r c", j=J, r=H)

        s_x, s_cst, s_wom, s_sel, s_rows = sem("s_x"), sem("s_cst"), sem("s_wom"), sem("s_sel"), sem("s_rows")
        s_zero = sem("s_zero")
        s_sum, s_mean, s_sq, s_var, s_eps, s_rstd = (sem(n) for n in
                                                     ("s_sum", "s_mean", "s_sq", "s_var", "s_eps", "s_rstd"))
        s_pool, s_qkv, s_ev, s_chans = sem("s_pool"), sem("s_qkv"), sem("s_ev"), sem("s_chans")
        s_up, s_hid, s_down, s_gate = sem("s_up"), sem("s_hid"), sem("s_down"), sem("s_gate")
        s_prod, s_log, s_dlog, s_exp, s_prob, s_hi, s_lo = (sem(n) for n in (
            "s_prod", "s_log", "s_dlog", "s_exp", "s_prob", "s_hi", "s_lo"))
        s_pb, s_pv, s_att, s_attn, s_proj = (sem(n) for n in ("s_pb", "s_pv", "s_att", "s_attn", "s_proj"))
        s_dve = sem("s_dve")
        s_x2, s_x2seq = sem("s_x2"), sem("s_x2seq")
        s_img2, s_tall = sem("s_img2"), sem("s_tall")
        s_conv, s_omraw, s_om, s_parts, s_stack = (sem(n) for n in ("s_conv", "s_omraw", "s_om", "s_parts", "s_stack"))
        s_amax, s_amaxT, s_choice = sem("s_amax"), sem("s_amaxT"), sem("s_choice")
        s_mb, s_mask = sem("s_mb"), sem("s_mask")
        s_staged, s_tr, s_xTa, s_xTd, s_xs, s_ybias = (sem(n) for n in (
            "s_staged", "s_tr", "s_xTa", "s_xTd", "s_xs", "s_ybias"))
        s_selx, s_sely, s_absx, s_absy, s_ux, s_uy = (sem(n) for n in (
            "s_selx", "s_sely", "s_absx", "s_absy", "s_ux", "s_uy"))
        s_cx, s_cy, s_hatx, s_haty = sem("s_cx"), sem("s_cy"), sem("s_hatx"), sem("s_haty")
        s_bx, s_by, s_hx, s_smp, s_smpfree = (sem(n) for n in ("s_bx", "s_by", "s_hx", "s_smp", "s_smpfree"))
        s_vals, s_fin, s_acc, s_y, s_out = (sem(n) for n in ("s_vals", "s_fin", "s_acc", "s_y", "s_out"))

        ONE = 1
        FROM_ONE = [s_tr, s_smpfree, s_hatx, s_haty, s_smp, s_absx, s_absy, s_hx, s_acc]

        block = ctx.enter_context(nc.Block())

        NPART = 9

        @block.sync
        def _(sp):
            sp.dma_start(xin[:, :], x).then_inc(s_x, 16)
            at = 0
            for name, n in CONSTS:
                sp.dma_start(cst[name][:, :], cf[:, at:at + n]).then_inc(s_cst, 16)
                at += n
            sp.dma_start(bias[:, :], biases).then_inc(s_cst, 16)
            sp.dma_start(table[:, :], tables).then_inc(s_cst, 16)
            sp.dma_start(womt[:, :], wom).then_inc(s_wom, 16)
            sp.wait_ge(s_x2, 1)
            for h in range(HALVES):
                sp.dma_start(x2seq[:, :].rearrange("c (j h n) -> c j h n", j=J, h=HALVES)[:, :, h, :],
                             images(x2)[h * C:(h + 1) * C]).then_inc(s_x2seq, 16)
            sp.wait_ge(s_parts, 1)
            for i in range(3):
                for n, k in enumerate("myx"):
                    sp.dma_start(stack[k][i * ND:(i + 1) * ND, :], part[i][n * ND:(n + 1) * ND, :]).then_inc(s_stack, 16)
            sp.wait_ge(s_y, 1)
            sp.dma_start(out, x2seq[:, :]).then_inc(s_out, 16)
            sp.wait_ge(s_out, 16)

        ZEROS = 8

        @block.gpsimd
        def _(pool):
            pool.dma_start(bcast[:, :], sel16["bcast"]).then_inc(s_sel, 16)
            for name, n in SELS:
                pool.dma_start(sel[name][:, :].bitcast(u16), sel16[name]).then_inc(s_sel, 16)
            for k in "ymx":
                pool.dma_start(stack[k][STACK:STACK + 2, :].bitcast(u16), rows16["x" if k == "x" else "y"]).then_inc(s_rows, 16)
            for counter in FROM_ONE:
                pool.sem_inc(counter, ONE)
            nc.gpsimd.memset(img[:, :], 0.0).then_inc(s_zero, 1)
            nc.gpsimd.memset(minushalf[:, :], -0.5).then_inc(s_zero, 1)
            nc.gpsimd.memset(one[:, :], 1.0).then_inc(s_zero, 1)
            nc.gpsimd.memset(hsum[:, :], 0.0).then_inc(s_zero, 1)
            nc.gpsimd.memset(kpad[:, :], 0.0).then_inc(s_zero, 1)
            nc.gpsimd.memset(vpad[:, :], 0.0).then_inc(s_zero, 1)
            pool.wait_ge(s_eps, 1)
            pool.wait_ge(s_zero, 6)
            nc.gpsimd.tensor_tensor(rstd[:, :], stat[:, 2 * J:3 * J], minushalf[:, :], ALU.pow).then_inc(s_rstd, 1)
            nc.gpsimd.memset(acc[:, :], 0.0).then_inc(s_zero, 1)
            pool.wait_ge(s_x2, 1)
            nc.gpsimd.memset(tall[:, :], 0.0).then_inc(s_zero, 1)
            for i in range(2):
                nc.gpsimd.memset(xs[i][:, :], 0.0).then_inc(s_zero, 1)
            nc.gpsimd.memset(vals[1][:, :], 0.0).then_inc(s_vals, 1)
            pool.wait_ge(s_eps, 2)
            nc.gpsimd.tensor_tensor(rstd[:, :], stat[:, 2 * J:3 * J], minushalf[:, :], ALU.pow).then_inc(s_rstd, 1)
            pool.wait_ge(s_zero, 10)
            pool.wait_ge(s_img2, 1)
            nc.gpsimd.tensor_copy(
                tall[:, :].rearrange("p (j r c) -> p j r c", j=J, r=TROWS)[:, :, -FIRST_ROW:-FIRST_ROW + H, :],
                shifted(img, 4)).then_inc(s_tall, 1)
            pool.wait_ge(s_tall, 1)

            pool.wait_ge(s_choice, 1)
            passes = pool.value_load(choice[0:1, 0:1], min_val=1, max_val=SHIFTS)
            shift0 = pool.value_load(choice[0:1, 1:2], min_val=0, max_val=SHIFTS // 2)

            def spread(i, src_j, h, first=False):
                src = xT[:, bass.ds(src_j * (WINS * P), WINS * P)].rearrange(
                    "p (w h g c) -> p w h g c", w=WINS, h=HALVES, g=DG)[:, :, h, :, :]
                dst = xs[i][:, :].rearrange("p (w g c) -> p w g c", w=WINS, g=DG)[:, :, :, CG:2 * CG]
                if first:
                    ones = one[:, :].unsqueeze(2).unsqueeze(3).to_broadcast([P, WINS, DG, CG])
                    return nc.gpsimd.tensor_tensor(dst, src, ones, ALU.mult)
                return nc.gpsimd.tensor_copy(dst, src)

            def low_parts(p, n):
                t = 2 * p
                w = HW * min(2, TAPS - t)
                pool.wait_ge(s_cx, n)
                pool.wait_ge(s_haty, ONE + (n - 1) * 2)
                nc.gpsimd.tensor_tensor(hatx[C:P, t * HW:t * HW + w], distx[C:P, 0:w], hatx[C:P, t * HW:t * HW + w],
                                        ALU.subtract).then_inc(s_hatx, 1)
                pool.wait_ge(s_cy, n)
                pool.wait_ge(s_hatx, ONE + n)
                for i, base in enumerate((32, 96)):
                    if i:
                        pool.wait_ge(s_haty, ONE + (n - 1) * 2 + 1)
                    nc.gpsimd.tensor_tensor(haty[base:base + 32, p * HW:(p + 1) * HW], disty[base:base + 32, :],
                                            haty[base:base + 32, p * HW:(p + 1) * HW],
                                            ALU.subtract).then_inc(s_haty, 1)

            with pool.Fori(0, passes) as it:
                pool.wait_ge(s_haty, ONE + it * (HP * 2))
                pool.wait_ge(s_tr, ONE + it * (WINS * J // 4))
                nc.gpsimd.tensor_copy(
                    images(staged), images(tall)[:, :, bass.ds(nc.s_assert_within(it + shift0, 0, SHIFTS - 1) * (WROWS * W), SROWS * W)]
                ).then_inc(s_staged, 1)
                pool.wait_ge(s_xTa, (it + 1) * 6)
                pool.wait_ge(s_xTd, (it + 1) * 6)
                pool.wait_ge(s_smpfree, ONE + it * (UNITS * B))
                spread(0, 0, 0, first=True).then_inc(s_xs, 1)
                pool.wait_ge(s_xs, it * (B + 1) + 1)
                for p in range(PAIRS):
                    low_parts(p, it * HP + p + 1)
                with pool.Fori(0, J) as j:
                    for h in range(HALVES):
                        pool.wait_ge(s_smpfree, ONE + it * (UNITS * B) + j * (2 * UNITS) + h * UNITS)
                        pool.wait_ge(s_haty, ONE + (it * HP + j * (2 * PAIRS) + (h + 1) * PAIRS) * 2)
                        spread(1 - h, j + h, 1 - h).then_inc(s_xs, 1)
                        pool.wait_ge(s_xs, it * (B + 1) + j * 2 + (h + 2))
                        for p in range(PAIRS):
                            low_parts(p, it * HP + j * (2 * PAIRS) + ((h + 1) * PAIRS + p + 1))

        @block.scalar
        def _(act):
            act.wait_ge(s_cst, 16 * (len(CONSTS) + 2))
            act.wait_ge(s_zero, 6)
            for t, (dst, src) in enumerate([(grid(q[:, :]), 0), (shifted(kpad, 4), 2)]):
                act.wait_ge(s_qkv, t + 1)
                nc.scalar.activation(dst, grid(bank(src, 2)), ACT.Identity, bias=bias[:, t:t + 1],
                                     scale=1.0 / TAPS).then_inc(s_ev, 1)
            act.wait_ge(s_up, 1)
            nc.scalar.activation(hidden[:, :], bank(6, 2), ACT.Relu, bias=bias[:, 4:5]).then_inc(s_hid, 1)
            act.wait_ge(s_down, 1)
            nc.scalar.activation(gate[:, :], bank(6, 2), ACT.Tanh, bias=b2half[:, :], scale=0.5).then_inc(s_gate, 1)
            act.wait_ge(s_dlog, 1)
            nc.scalar.activation(dlog[:, :], dlog[:, :], ACT.Exp, scale=SCALE).then_inc(s_exp, 1)
            act.wait_ge(s_prob, 1)
            nc.scalar.copy(prob16[:, :], dlog[:, :]).then_inc(s_hi, 1)
            for c in range(4):
                act.wait_ge(s_conv, c + 1)
                nc.scalar.activation(om[:, c * BANK:(c + 1) * BANK], bank(4 + c)[0:OM], ACT.Identity,
                                     bias=bias[0:OM, 7:8]).then_inc(s_omraw, 1)
            act.wait_ge(s_omraw, 4)
            nc.scalar.activation(om[0:ND, :], om[0:ND, :], ACT.Tanh, scale=0.5).then_inc(s_om, 1)
            for p in range(PAIRS):
                act.wait_ge(s_mb, p + 1)
                nc.scalar.copy(maskb[:, p * ALL:(p + 1) * ALL], bank(4 * (p % 2), 4)).then_inc(s_mask, 1)
            act.wait_ge(s_choice, 1)
            passes = act.value_load(choice[0:1, 0:1], min_val=1, max_val=SHIFTS)

            def evac(slot, n, bank_, w, waits_smp):
                act.wait_ge(s_bx, n)
                act.wait_ge(s_smp, ONE + waits_smp)
                nc.scalar.copy(hx[:, slot * BANK:slot * BANK + w], bank(bank_)[:, 0:w]).then_inc(s_hx, 1)

            def absolute(p, n):
                w = HW * min(2, TAPS - 2 * p)
                act.wait_ge(s_selx, n)
                act.wait_ge(s_hatx, ONE + n - 1)
                nc.scalar.activation(distx[:, 0:w], bank(5)[:, 0:w], ACT.Abs).then_inc(s_absx, 1)
                act.wait_ge(s_sely, n)
                act.wait_ge(s_haty, ONE + (n - 1) * 2)
                nc.scalar.activation(disty[:, :], bank(7)[:, 0:HW], ACT.Abs, bias=ybias[:, :]).then_inc(s_absy, 1)

            def cast(p, n):
                t = 2 * p
                w = HW * min(2, TAPS - t)
                act.wait_ge(s_ux, n)
                nc.scalar.copy(hatx[:, t * HW:t * HW + w], distx[:, 0:w]).then_inc(s_cx, 1)
                act.wait_ge(s_uy, n)
                nc.scalar.copy(haty[:, p * HW:(p + 1) * HW], disty[:, :]).then_inc(s_cy, 1)

            with act.Fori(0, passes) as it:
                for g in range(0, 12, 2):
                    act.wait_ge(s_tr, ONE + it * 12 + (g + 1))
                    nc.scalar.copy(xT[:, g * BANK:(g + 1) * BANK], bank(g % 4)).then_inc(s_xTa, 1)
                act.wait_ge(s_ybias, it + 1)
                for p in range(PAIRS):
                    absolute(p, it * HP + p + 1)
                    cast(p, it * HP + p + 1)
                for g in range(AHEAD):
                    evac(g, it * UP + g + 1, g % 2, BANK, it * UP)
                with act.Fori(0, J) as j:
                    for h in range(HALVES):
                        for u in range(UNITS):
                            g = h * UNITS + u + AHEAD
                            p = (u + AHEAD) % UNITS // DG
                            evac(g % 4, it * UP + j * (2 * UNITS) + g + 1, g % 2, HW * min(2, TAPS - 2 * p),
                                 it * UP + j * (2 * UNITS) + max(g - 3, 0))
                            n = it * HP + j * (2 * PAIRS) + ((h + 1) * PAIRS + u // 4 + 1)
                            if u % 4 == 2:
                                absolute(u // 4, n)
                            if u % 4 == 3:
                                cast(u // 4, n)

        @block.vector
        def _(dve):
            chain = [0]

            def link(ins):
                chain[0] += 1
                ins.then_inc(s_dve, 1)
                dve.wait_ge(s_dve, chain[0])

            def norm(src, dst, first):
                n = 1 if first else 2
                nc.vector.tensor_reduce(stat[:, 0:J], images(src), AX.X, ALU.add).then_inc(s_sum, 1)
                dve.wait_ge(s_mean, n)
                mean = bank(7)[:, 0:J].unsqueeze(2).to_broadcast([P, J, HW])
                link(nc.vector.tensor_tensor(images(xc), images(src), mean, ALU.subtract))
                link(nc.vector.tensor_tensor(sq[:, :], xc[:, :], xc[:, :], ALU.mult))
                nc.vector.tensor_reduce(stat[:, J:2 * J], images(sq), AX.X, ALU.add).then_inc(s_sq, 1)
                dve.wait_ge(s_var, n)
                nc.vector.tensor_scalar(stat[:, 2 * J:3 * J], bank(7)[:, J:2 * J], EPS, None, ALU.add).then_inc(s_eps, 1)
                dve.wait_ge(s_rstd, n)
                scale = rstd[:, :].unsqueeze(2).unsqueeze(3).to_broadcast([P, J, H, W])
                return nc.vector.tensor_tensor(dst, grid(xc[:, :]), scale, ALU.mult)

            dve.wait_ge(s_x, 16)
            dve.wait_ge(s_zero, 4)
            link(norm(xin, shifted(img, 4), True))
            im = padded(img)
            hs = hsum[:, :].rearrange("p (j r c) -> p j r c", j=J, r=PH)
            mid = hs[:, :, 1:H + 1, :]
            link(nc.vector.tensor_tensor(mid, im[:, :, 1:H + 1, 0:W], im[:, :, 1:H + 1, 1:W + 1], ALU.add))
            link(nc.vector.tensor_tensor(mid, mid, im[:, :, 1:H + 1, 2:W + 2], ALU.add))
            po = grid(pooled[:, :])
            link(nc.vector.tensor_tensor(po, hs[:, :, 0:H, :], hs[:, :, 1:H + 1, :], ALU.add))
            nc.vector.tensor_tensor(po, po, hs[:, :, 2:H + 2, :], ALU.add).then_inc(s_pool, 1)
            dve.wait_ge(s_cst, 16 * (len(CONSTS) + 2))
            nc.vector.tensor_scalar(b2half[:, :], bias[:, 5:6], 0.5, None, ALU.mult).then_inc(s_chans, 1)
            dve.wait_ge(s_zero, 6)
            dve.wait_ge(s_qkv, 3)
            nc.vector.tensor_scalar(shifted(vpad, 4), grid(bank(4, 2)), 1.0 / TAPS, bias[:, 2:3], ALU.mult,
                                    ALU.add).then_inc(s_ev, 1)
            dve.wait_ge(s_qkv, 4)
            nc.vector.tensor_scalar(chans[:, :], bank(6, 2), 1.0 / TAPS, bias[:, 3:4], ALU.mult,
                                    ALU.add).then_inc(s_chans, 1)
            dve.wait_ge(s_ev, 3)
            for t in range(TAPS):
                nc.vector.tensor_tensor(grid(prod[:, t * N:(t + 1) * N]), grid(q[:, :]), shifted(kpad, t),
                                        ALU.mult).then_inc(s_prod, 1)
            dve.wait_ge(s_gate, 1)
            link(nc.vector.tensor_scalar(gate[:, :], gate[:, :], 0.5, 1.5, ALU.mult, ALU.add))
            dve.wait_ge(s_log, TAPS)
            logits = ps[:, 0:TAPS * HW].rearrange("p (t n) -> p t n", t=TAPS)
            link(nc.vector.tensor_reduce(lmax[:, :], logits.rearrange("p t n -> p n t"), AX.X, ALU.max))
            d3 = dlog[:, :].rearrange("p (t n) -> p t n", t=TAPS)
            nc.vector.tensor_tensor(d3, logits, lmax[:, :].unsqueeze(1).to_broadcast([P, TAPS, HW]),
                                    ALU.subtract).then_inc(s_dlog, 1)
            dve.wait_ge(s_exp, 1)
            link(nc.vector.tensor_reduce(den[:, :], d3.rearrange("p t n -> p n t"), AX.X, ALU.add))
            link(nc.vector.reciprocal(den[:, :], den[:, :]))
            nc.vector.tensor_tensor(d3, d3, den[:, :].unsqueeze(1).to_broadcast([P, TAPS, HW]),
                                    ALU.mult).then_inc(s_prob, 1)
            dve.wait_ge(s_hi, 1)
            dve.wait_ge(s_prob, 1)
            nc.vector.tensor_tensor(prob16[C:P, :], dlog[C:P, :], prob16[C:P, :], ALU.subtract).then_inc(s_lo, 1)
            for t in range(TAPS):
                dve.wait_ge(s_pb, t + 1)
                nc.vector.tensor_tensor(grid(prod[:, t * N:(t + 1) * N]), grid(bank(4 + 2 * (t % 2), 2)),
                                        shifted(vpad, t), ALU.mult).then_inc(s_pv, 1)
            dve.wait_ge(s_att, 1)
            nc.vector.tensor_tensor(att[:, :], bank(2, 2), gate[:, :], ALU.mult).then_inc(s_attn, 1)
            dve.wait_ge(s_proj, 1)
            nc.vector.scalar_tensor_tensor(x2[:, :], bank(0, 2), bias[:, 6:7], xin[:, :], ALU.add,
                                           ALU.add).then_inc(s_x2, 1)
            dve.wait_ge(s_x2, 1)
            norm(x2, shifted(img, 4), False).then_inc(s_img2, 1)
            dve.wait_ge(s_om, 1)
            link(nc.vector.tensor_reduce(amax[:, :], om[:, :], AX.X, ALU.max, apply_absolute_value=True))
            nc.vector.tensor_scalar(amax[:, :], amax[:, :], 1.0, None, ALU.mult).then_inc(s_amax, 1)
            link(nc.vector.tensor_copy(part[0][:, :], om[:, :]))
            link(nc.vector.tensor_tensor(rest[:, :], om[:, :], part[0][:, :], ALU.subtract))
            link(nc.vector.tensor_copy(part[1][:, :], rest[:, :]))
            nc.vector.tensor_tensor(part[2][:, :], rest[:, :], part[1][:, :], ALU.subtract).then_inc(s_parts, 1)
            dve.wait_ge(s_amaxT, 1)
            link(nc.vector.tensor_reduce(far[0:1, 0:1], bank(3)[0:1, 0:OM], AX.X, ALU.max))
            link(nc.vector.tensor_scalar(far[0:1, 1:2], far[0:1, 0:1], float(REACH), float(SHIFTS // 2), ALU.is_gt,
                                         ALU.mult))
            nc.vector.tensor_scalar(choice[0:1, 0:1], far[0:1, 1:2], 2.0, 1.0, ALU.mult, ALU.add)
            nc.vector.tensor_scalar(choice[0:1, 1:2], far[0:1, 1:2], -1.0, float(SHIFTS // 2), ALU.mult,
                                    ALU.add).then_inc(s_choice, 1)
            dve.wait_ge(s_choice, 1)
            passes = dve.value_load(choice[0:1, 0:1], min_val=1, max_val=SHIFTS)
            shift0 = dve.value_load(choice[0:1, 1:2], min_val=0, max_val=SHIFTS // 2)
            dve.wait_ge(s_zero, 10)
            dve.wait_ge(s_mask, PAIRS)
            dve.wait_ge(s_x2seq, 16 * HALVES)

            def distance_to_hat(p, n):
                w = HW * min(2, TAPS - 2 * p)
                dve.wait_ge(s_absx, ONE + n)
                nc.vector.tensor_scalar(distx[:, 0:w], distx[:, 0:w], 1.0, 1.0, ALU.min, ALU.subtract).then_inc(s_ux, 1)
                dve.wait_ge(s_absy, ONE + n)
                nc.vector.tensor_scalar(disty[:, :], disty[:, :], 1.0, 1.0, ALU.min, ALU.subtract).then_inc(s_uy, 1)

            def sample(g, w, n, nfree):
                s = g % 4
                dve.wait_ge(s_by, n)
                dve.wait_ge(s_hx, ONE + n)
                dve.wait_ge(s_smpfree, ONE + nfree)
                nc.vector.tensor_tensor(smp[:, s * BANK:s * BANK + w], bank(2 + g % 2)[:, 0:w],
                                        hx[:, s * BANK:s * BANK + w], ALU.mult).then_inc(s_smp, 1)

            def accumulate(slot, n):
                dve.wait_ge(s_fin, n)
                dve.wait_ge(s_acc, ONE + n - 1)
                a = acc[:, bass.ds(slot * HW, HW)]
                nc.vector.tensor_tensor(a, bank(7)[0:C, 0:HW], a, ALU.add).then_inc(s_acc, 1)

            with dve.Fori(0, passes) as it:
                dve.wait_ge(s_absy, ONE + it * HP)
                nc.vector.tensor_copy(ybias[:, :], table[:, bass.ds(nc.s_assert_within(it + shift0, 0, SHIFTS - 1), 1)]).then_inc(s_ybias, 1)
                for g in range(1, 12, 2):
                    dve.wait_ge(s_tr, ONE + it * 12 + (g + 1))
                    nc.vector.tensor_copy(xT[:, g * BANK:(g + 1) * BANK], bank(g % 4)).then_inc(s_xTd, 1)
                for p in range(PAIRS):
                    distance_to_hat(p, it * HP + p + 1)
                for g in range(AHEAD):
                    sample(g, BANK, it * UP + g + 1, it * (UNITS * B))
                with dve.Fori(0, J) as j:
                    for h in range(HALVES):
                        for u in range(UNITS):
                            g = h * UNITS + u + AHEAD
                            p = (u + AHEAD) % UNITS // DG
                            sample(g, HW * min(2, TAPS - 2 * p), it * UP + j * (2 * UNITS) + g + 1,
                                   it * (UNITS * B) + j * (2 * UNITS) + max(g - 3, 0))
                            if u % 4 == 3:
                                p = u // 4
                                distance_to_hat(p, it * HP + j * (2 * PAIRS) + ((h + 1) * PAIRS + p + 1))
                                dve.wait_ge(s_smpfree, ONE + it * (UNITS * B) + j * (2 * UNITS) + (h * UNITS + u + 1))
                                nc.vector.tensor_tensor(
                                    vals[h][:, p * HW:(p + 1) * HW], bank(4 + 2 * ((h + p) % 2))[:, 0:HW],
                                    maskb[:, bass.ds(j * HW + (p * ALL + h * N), HW)], ALU.mult).then_inc(s_vals, 1)
                            if u == 4:
                                accumulate(j * 2 + h, it * (B + 1) + j * 2 + (h + 1))
                accumulate(B, it * (B + 1) + (B + 1))
            dve.wait_ge(s_acc, ONE + passes * (B + 1))
            nc.vector.scalar_tensor_tensor(x2seq[:, :], acc[:, HW:], 0.0, x2seq[:, :], ALU.max, ALU.add).then_inc(s_y, 1)

        @block.tensor
        def _(pe):
            def pairsum(src, dst, n):
                return nc.tensor.matmul(bank(7)[:, dst:dst + J], gnp[:, :], stat[:, src:src + J], start=True, stop=True)

            def dense(dst, w, src, signal):
                for c in range(2):
                    ins = nc.tensor.matmul(bank(dst + c), w, src[:, c * BANK:(c + 1) * BANK], start=True, stop=True)
                ins.then_inc(signal, 1)

            pe.wait_ge(s_cst, 16 * (len(CONSTS) + 2))
            pe.wait_ge(s_sum, 1)
            pairsum(0, 0, 1).then_inc(s_mean, 1)
            pe.wait_ge(s_sq, 1)
            pairsum(J, J, 1).then_inc(s_var, 1)
            pe.wait_ge(s_pool, 1)
            for t in range(4):
                dense(2 * t, cst["wqkv"][:, t * P:(t + 1) * P], pooled, s_qkv)
            pe.wait_ge(s_chans, 2)
            dense(6, cst["w1"][:, :], chans, s_up)
            pe.wait_ge(s_hid, 1)
            dense(6, cst["w2"][:, :], hidden, s_down)
            pe.wait_ge(s_ev, 3)
            for t in range(TAPS):
                pe.wait_ge(s_prod, t + 1)
                for j in range(J):
                    ins = nc.tensor.matmul(ps[:, t * HW:(t + 1) * HW], cst["headsum"][:, j * P:(j + 1) * P],
                                           prod[:, t * N + j * HW:t * N + (j + 1) * HW], start=(j == 0), stop=(j == J - 1))
                ins.then_inc(s_log, 1)
            pe.wait_ge(s_gate, 1)
            pe.wait_ge(s_sel, 16 * 4)
            pe.wait_ge(s_lo, 1)

            def spread_probs(t):
                if t >= 2:
                    pe.wait_ge(s_pv, t - 1)
                for j in range(J):
                    c = (3 * DG + j) * P
                    ins = nc.tensor.matmul(ps[:, (4 + 2 * (t % 2)) * BANK + j * HW:][:, 0:HW], bcast[:, c:c + P],
                                           prob16[:, t * HW:(t + 1) * HW], start=True, stop=True)
                ins.then_inc(s_pb, 1)

            spread_probs(0)
            for t in range(TAPS):
                if t + 1 < TAPS:
                    spread_probs(t + 1)
                pe.wait_ge(s_pv, t + 1)
                for c in range(2):
                    ins = nc.tensor.matmul(bank(2 + c), ident[:, :], prod[:, t * N + c * BANK:][:, 0:BANK],
                                           start=(t == 0), stop=(t == TAPS - 1))
            ins.then_inc(s_att, 1)
            pe.wait_ge(s_attn, 1)
            dense(0, cst["wp"][:, :], att, s_proj)
            pe.wait_ge(s_sum, 2)
            pairsum(0, 0, 2).then_inc(s_mean, 1)
            pe.wait_ge(s_sq, 2)
            pairsum(J, J, 2).then_inc(s_var, 1)
            pe.wait_ge(s_wom, 16)
            pe.wait_ge(s_img2, 1)
            for c in range(4):
                h, j = c // 2, c % 2 * 2
                for t in range(TAPS):
                    at = (h * TAPS + t) * OM
                    ins = nc.tensor.matmul(bank(4 + c)[0:OM], womt[:, at:at + OM], shifted(img, t)[:, j:j + 2],
                                           start=(t == 0), stop=(t == TAPS - 1))
                ins.then_inc(s_conv, 1)
            pe.wait_ge(s_amax, 1)
            nc.tensor.matmul(bank(3)[0:1, 0:OM], amax[:, :], ident[0:OM, 0:OM], start=True, stop=True).then_inc(s_amaxT, 1)
            pe.wait_ge(s_choice, 1)
            pe.wait_ge(s_stack, 16 * NPART)
            pe.wait_ge(s_rows, 16 * 3)
            pe.wait_ge(s_omraw, 4)
            for p in range(PAIRS):
                if p >= 2:
                    pe.wait_ge(s_mask, p - 1)
                for c in range(4):
                    ins = nc.tensor.matmul(bank(4 * (p % 2) + c), sel["selm"][:, p * P:(p + 1) * P],
                                           stack["m"][:, c * BANK:(c + 1) * BANK], start=True, stop=True)
                ins.then_inc(s_mb, 1)
            pe.wait_ge(s_mask, PAIRS)
            passes = pe.value_load(choice[0:1, 0:1], min_val=1, max_val=SHIFTS)

            def select(p, image, n, nacc):
                cols = bass.ds(image * HW, HW)
                pe.wait_ge(s_absx, ONE + n - 1)
                for t in range(2 * p, min(2 * p + 2, TAPS)):
                    ins = nc.tensor.matmul(bank(5)[:, t % 2 * HW:(t % 2 + 1) * HW], sel["selx"][:, t * P:(t + 1) * P],
                                           stack["x"][:, cols], start=True, stop=True)
                ins.then_inc(s_selx, 1)
                pe.wait_ge(s_absy, ONE + n - 1)
                pe.wait_ge(s_acc, ONE + nacc)
                nc.tensor.matmul(bank(7)[:, 0:HW], sel["sely"][:, p * P:(p + 1) * P], stack["y"][:, cols],
                                 start=True, stop=True).then_inc(s_sely, 1)

            def issue(g, unit, nhat, n):
                p, d = unit // DG, unit % DG
                taps = min(2, TAPS - 2 * p)
                if d == 0:
                    pe.wait_ge(s_hatx, ONE + nhat)
                    pe.wait_ge(s_haty, ONE + nhat * 2)
                pe.wait_ge(s_hx, ONE + n)
                nc.tensor.matmul(bank(g % 2)[:, 0:taps * HW], bcast[:, d * P:(d + 1) * P],
                                 hatx[:, 2 * p * HW:(2 * p + taps) * HW], start=True, stop=True).then_inc(s_bx, 1)
                pe.wait_ge(s_smp, ONE + n)
                for a in range(taps):
                    at = (DG + 2 * d + a) * P
                    ins = nc.tensor.matmul(bank(2 + g % 2)[:, a * HW:(a + 1) * HW], bcast[:, at:at + P],
                                           haty[:, p * HW:(p + 1) * HW], start=True, stop=True)
                ins.then_inc(s_by, 1)

            def products(h, u, n, nv):
                p, d = u // DG, u % DG
                taps = min(2, TAPS - 2 * p)
                if d == 0:
                    pe.wait_ge(s_vals, nv)
                pe.wait_ge(s_smp, ONE + n)
                slot = bank(4 + 2 * ((h + p) % 2))
                sm = (h * UNITS + u) % 4 * BANK
                for a in range(taps):
                    for s in range(STRIPS):
                        w = ((s * 3 + (2 * p + a) // 3) * DG + d) * XSW + (CG if a == 0 else 0)
                        o = s * STRIP * W
                        m = sm + a * HW + s * STRIP * W
                        ins = nc.tensor.matmul(slot[32 * d:32 * d + 32, o:o + STRIP * W], xs[h][:, w:w + 2 * CG],
                                               smp[:, m:m + STRIP * W], start=(a == 0 and s == 0),
                                               stop=(a == taps - 1), skip_group_check=True)
                ins.then_inc(s_smpfree, 1)
                return ins

            def final(i, n, nv, ny):
                pe.wait_ge(s_vals, nv)
                pe.wait_ge(s_absy, ONE + ny)
                pe.wait_ge(s_acc, ONE + n - 1)
                for p in range(PAIRS):
                    ins = nc.tensor.matmul(bank(7)[0:C, 0:HW], cst["wfin"][:, p * C:(p + 1) * C],
                                           vals[i][:, p * HW:(p + 1) * HW], start=(p == 0), stop=(p == PAIRS - 1))
                ins.then_inc(s_fin, 1)

            with pe.Fori(0, passes) as it:
                pe.wait_ge(s_staged, it + 1)
                pe.wait_ge(s_smp, ONE + it * UP)
                pe.wait_ge(s_hx, ONE + it * UP)
                for g in range(12):
                    if g >= 4:
                        if g % 2 == 0:
                            pe.wait_ge(s_xTa, it * 6 + (g - 4) // 2 + 1)
                        else:
                            pe.wait_ge(s_xTd, it * 6 + (g - 5) // 2 + 1)
                    for k in range(4):
                        j, w = divmod(4 * g + k, WINS)
                        row = w // 3 * STRIP + w % 3
                        ins = nc.tensor.transpose(bank(g % 4)[:, k * P:(k + 1) * P],
                                                  images(staged)[:, j, row * W:(row + WROWS) * W], ident[:, :])
                    ins.then_inc(s_tr, 1)
                for p in range(PAIRS):
                    select(p, 0, it * HP + p + 1, it * (B + 1))
                pe.wait_ge(s_xTa, (it + 1) * 6)
                pe.wait_ge(s_xTd, (it + 1) * 6)
                for g in range(AHEAD):
                    issue(g, g, it * HP + 1, it * UP)
                with pe.Fori(0, J) as j:
                    for h in range(HALVES):
                        pe.wait_ge(s_xs, it * (B + 1) + j * 2 + (h + 1))
                        for u in range(UNITS):
                            g = h * UNITS + u + AHEAD
                            nxt, unit = divmod(u + AHEAD, UNITS)
                            issue(g, unit, it * HP + j * (2 * PAIRS) + ((h + nxt) * PAIRS + unit // DG + 1),
                                  it * UP + j * (2 * UNITS) + (g - 1))
                            if u % 4 == 1:
                                select(u // 4, j + (J if h == 0 else 1),
                                       it * HP + j * (2 * PAIRS) + ((h + 1) * PAIRS + u // 4 + 1),
                                       it * (B + 1) + j * 2 + h + (u > 4))
                            products(h, u, it * UP + j * (2 * UNITS) + (h * UNITS + u + 1),
                                     it * (PAIRS * B) + j * (2 * PAIRS) + (h * PAIRS + u // DG))
                            if u == 3:
                                final(1 - h, it * (B + 1) + j * 2 + (h + 1),
                                      it * (PAIRS * B) + j * (2 * PAIRS) + (h * PAIRS + 1),
                                      it * HP + j * (2 * PAIRS) + ((h + 1) * PAIRS + 1))
                final(1, it * (B + 1) + (B + 1), it * (PAIRS * B) + (PAIRS * B + 1), (it + 1) * HP)


def _layout(a):
    import numpy as np

    def diag(w):
        o = np.zeros((HALVES * w.shape[0], HALVES * w.shape[1]), np.float32)
        for h in range(HALVES):
            o[h * w.shape[0]:(h + 1) * w.shape[0], h * w.shape[1]:(h + 1) * w.shape[1]] = w
        return np.pad(o, ((0, P - o.shape[0]), (0, P - o.shape[1])))

    def rows(v):
        v = np.concatenate([v] * HALVES)
        return np.pad(v, (0, P - v.shape[0]))

    i = np.arange(P)
    gnp = np.where(i[:, None] // GC == i[None] // GC, 1.0 / (GC * HW), 0.0)
    wq = a["L0_conv_W_qkv"].reshape(C, 4, C)
    headsum = np.zeros((P, J, P))
    spread = np.zeros((P, J, P))
    for j in range(J):
        for p in range(P):
            r = j * 16 + p // C * HEADS + p % C // HD
            headsum[p, j, r] = headsum[p, j, r + C] = 1
            spread[r, j, p] = spread[r + C, j, p] = 1
    wd = a["L1_conv_w_dcn"].reshape(C, DG, CG, TAPS)
    wfin = np.zeros((DG, 2, CG, PAIRS, C), np.float32)
    for t in range(TAPS):
        wfin[:, t % 2, :, t // 2, :] = wd[:, :, :, t].transpose(1, 2, 0)
    cf = np.concatenate([gnp, np.eye(P), wfin.reshape(P, -1)] + [diag(wq[:, t].T) for t in range(4)] + [
        diag(a["L0_conv_W1"].T), diag(a["L0_conv_W2"].T), diag(a["L0_conv_Wp"].T), headsum.reshape(P, -1)], axis=1).astype(np.float32)

    order = [2 * ND + n for n in range(ND)] + [2 * n for n in range(ND)] + [2 * n + 1 for n in range(ND)]
    wo = a["L1_conv_w_om"][order].reshape(OM, C, TAPS).transpose(1, 2, 0)
    wom = np.zeros((HALVES, C, HALVES, TAPS, OM), np.float32)
    for h in range(HALVES):
        wom[h, :, h] = wo
    bq = a["L0_conv_b_qkv"].reshape(C, 4)
    bias = np.stack([rows(bq[:, t]) for t in range(4)] + [
        rows(a["L0_conv_b1"]), rows(a["L0_conv_b2"]), rows(a["L0_conv_bp"]),
        np.pad(a["L1_conv_b_om"][order], (0, P - OM))], axis=1)
    table = np.tile([-float(WROWS) * (s - SHIFTS // 2) for s in range(SHIFTS)], (P, 1)).astype(np.float32)

    sely, selx, selm = (np.zeros((STACK + 2, n, P), np.float32) for n in (PAIRS, TAPS, PAIRS))
    for t in range(TAPS):
        p, ab = divmod(t, 2)
        for d in range(DG):
            src = [i * ND + d * TAPS + t for i in range(3)]
            for part in range(2):
                for r in range(WROWS):
                    c = ab * 64 + part * 32 + d * WROWS + r
                    sely[src, p, c] = 1
                    sely[STACK, p, c] = 1
                    sely[STACK + 1, p, c] = -r
                for x in range(W):
                    c = part * 64 + d * W + x
                    selx[src, t, c] = 1
                    selx[STACK, t, c] = 1
                    selx[STACK + 1, t, c] = t % 3 - 1 - x
            c = slice(d * 32 + ab * CG, d * 32 + ab * CG + CG)
            selm[src, p, c] = 0.5
            selm[STACK + 1, p, c] = 0.5
    bx, by = np.zeros((P, DG, P)), np.zeros((P, DG, 2, P))
    for d in range(DG):
        for part in range(2):
            for m in range(P):
                bx[part * 64 + d * W + m % W, d, m] = 1
                for ab in range(2):
                    by[ab * 64 + part * 32 + d * WROWS + m // W, d, ab, m] = 1
    n = np.arange(ALL) % HW
    f16 = np.float16

    def bf16_bits(v):
        return (v.astype(np.float32).view(np.uint32) >> 16).astype(np.uint16)

    return {
        "x": a["x"].reshape(HALVES, J, C, HW).transpose(0, 2, 1, 3).reshape(P, N), "cf": cf,
        "wom": wom.reshape(P, -1), "biases": bias, "tables": table,
        "bcast": np.concatenate([bx.reshape(P, -1), by.reshape(P, -1), spread.reshape(P, -1)], 1).astype(f16),
        "sely": bf16_bits(sely.reshape(STACK + 2, -1)), "selx": bf16_bits(selx.reshape(STACK + 2, -1)),
        "selm": bf16_bits(selm.reshape(STACK + 2, -1)),
        "rowsy": bf16_bits(np.stack([n // W % STRIP + REACH, np.ones(ALL)])),
        "rowsx": bf16_bits(np.stack([n % W, np.ones(ALL)])),
    }


def kernel(**inputs):
    import numpy as np
    import concourse.bacc as bacc
    from concourse.bass_utils import run_bass_kernel_spmd as run

    arrays = {k: np.ascontiguousarray(v) for k, v in _layout({k: np.asarray(v) for k, v in inputs.items()}).items()}
    nc = bacc.Bacc("TRN2", target_bir_lowering=False, num_devices=1)
    d = {k: nc.dram_tensor("in_" + k, v.shape, mybir.dt.from_np(v.dtype), kind="ExternalInput").ap() for k, v in arrays.items()}
    out = nc.dram_tensor("out", (C, ALL), mybir.dt.float32, kind="ExternalOutput").ap()
    bass_local_attention_then_deformable_conv(
        nc, d["x"], d["cf"], d["wom"], d["biases"], d["tables"],
        {k: d[k] for k in ("bcast", "sely", "selx", "selm")}, {"y": d["rowsy"], "x": d["rowsx"]}, out)
    r = run(nc, [{"in_" + k: v for k, v in arrays.items()}], core_ids=[0])
    y = r.results[0]["out"].reshape(C, J, HALVES, H, W)
    return np.ascontiguousarray(y.transpose(2, 1, 0, 3, 4)).reshape(B, C, H, W)
```

```python
import concourse.bass as bass
from concourse import mybir
from contextlib import ExitStack

B, C, H, W = 8, 64, 16, 16
HW = H * W
HALVES = 2
J = B // HALVES
P = HALVES * C
N = J * HW
ALL = B * HW
TAPS = 9
PH, PW = H + 2, W + 2
HEADS, HD = 8, 8
SCALE = float(HD) ** -0.5
EPS = 1e-5
GC = 2
DG = 4
CG = C // DG
PAIRS = (TAPS + 1) // 2
OM = 3 * DG * TAPS
ND = DG * TAPS
STACK = 3 * ND
STRIP = 4
STRIPS = H // STRIP
WROWS = P // W
REACH = 2
SHIFTS = 5
WINS = 3 * STRIPS
SROWS = (STRIPS - 1) * STRIP + 2 + WROWS
FIRST_ROW = -(1 + REACH) - WROWS * (SHIFTS // 2)
TROWS = WROWS * (SHIFTS - 1) + SROWS
UNITS = PAIRS * DG
AHEAD = 2
AHEAD_X = 3
UP = UNITS * B + AHEAD
UPX = UNITS * B + AHEAD_X
HP = PAIRS * (B + 1)
BANK = 512
HF = HW // 2
CHUNKS = 3
TC = TAPS // CHUNKS
CONV = [0, 2, 1, 3]
TAPSTEPS = 6
CENTER = SHIFTS // 2
POOL_TAPS = 3


def bass_local_attention_then_deformable_conv(nc, x, cf, wom, sel16, rows16, out):
    fp32, bf16, fp16 = mybir.dt.float32, mybir.dt.bfloat16, mybir.dt.float16
    i32, u16 = mybir.dt.int32, mybir.dt.uint16
    ALU = mybir.AluOpType
    ACT = mybir.ActivationFunctionType
    AX = mybir.AxisListType
    KEPT = [("gnp", P), ("gnd", P), ("ident", P), ("wfin", PAIRS * C), ("bias", 8), ("table", SHIFTS)]
    ATTENTION = [("wqkv", 4 * P), ("w1", P), ("w2", P), ("wp", P), ("headsum", 2 * 32)]
    SELS = [("sely", PAIRS * P), ("selx", TAPS * P), ("selm", PAIRS * P)]

    with ExitStack() as ctx:
        def sb(name, shape, dt=fp32):
            return ctx.enter_context(nc.sbuf_tensor(name, shape, dt))

        def sem(name):
            return ctx.enter_context(nc.semaphore(name))

        kept = sb("kept", [P, sum(n for _, n in KEPT)])
        cst, at = {}, 0
        for name, n in KEPT:
            cst[name] = kept[:, at:at + n]
            at += n
        gnp, gnd, ident, bias, table = (cst[k] for k in ("gnp", "gnd", "ident", "bias", "table"))
        sel = {name: sb(f"s_{name}", [STACK + 2, n], bf16) for name, n in SELS}
        bcast = sb("bcast", [P, (DG + 2 * DG + 2 * J) * P], fp16)
        b2half = sb("b2half", [P, 1])
        minushalf = sb("minushalf", [P, J])
        halfstat = sb("halfstat", [P, 6 * J])
        meanvar = sb("meanvar", [P, 2 * J])
        pair = sb("pair", [P, 4 * J])
        one = sb("one", [P, 1])
        gap2 = sb("gap2", [P, J])
        vareps = sb("vareps", [P, J])
        rstd = sb("rstd", [P, J])

        PAD, XSW = J * PH * PW, 3 * CG

        def shared(name, first, then):
            size = max(sum(n for _, n in first), sum(n for _, n in then))
            words, views = sb(name, [P, size]), {}
            for names in (first, then):
                at = 0
                for key, n in names:
                    views[key] = words[:, at:at + n]
                    at += n
            return views

        W_ATT = sum(n for _, n in ATTENTION)
        m = shared("attention_weights", [("all", W_ATT)], [("vals1", PAIRS * HW)])
        attw, at = m["all"], 0
        for name, n in ATTENTION:
            cst[name] = attw[:, at:at + n]
            at += n
        m1 = shared("conv1_vals0", [("dup1", PAD)], [("vals0", PAIRS * HW)])
        vals = [m1["vals0"], m["vals1"]]
        m = shared("conv0_hx", [("womt", TAPSTEPS * OM), ("dup0", PAD)], [("hx", 4 * BANK)])
        womt, hx, dup = m["womt"], m["hx"], [m["dup0"], m1["dup1"]]
        m = shared("x_parts_smp", [("xin", N), ("x2", N)], [("smp", 4 * BANK)])
        xin, x2, smp = m["xin"], m["x2"], m["smp"]
        parts = smp[0:OM, 0:2 * 3 * BANK // 2].bitcast(bf16).rearrange("p (k i n) -> p k i n", k=2, i=3)
        rest = smp[0:OM, 2 * 3 * BANK // 2:2 * 3 * BANK // 2 + BANK]
        om = sb("om", [OM, 2 * BANK])
        m = shared("img_staged", [("img", PAD)], [("staged", J * SROWS * W)])
        img, staged = m["img"], m["staged"]
        m = shared("prod_maskb", [("prod", TAPS * N)], [("maskb", PAIRS * ALL)])
        prod, maskb = m["prod"], m["maskb"]

        WX, XS = J * WINS * P, WINS * DG * XSW
        arena = sb("arena", [P, WX + J * TROWS * W + 2 * XS])
        at = 0
        views = {}
        for key in ("pooled", "q", "chans", "hidden", "gate", "att"):
            views[key] = arena[:, at:at + N]
            at += N
        pooled, q, chans, hidden, gate, att = (views[k] for k in ("pooled", "q", "chans", "hidden", "gate", "att"))
        xT = arena[:, 0:WX + WINS * P]
        at = WX
        for key, n in (("kpad", PAD), ("vpad", PAD), ("hsum", J * PH * W), ("dlog", TAPS * HF), ("lmax", HF),
                       ("den", HF)):
            views[key] = arena[:, at:at + n]
            at += n
        kpad, vpad, hsum, dlog, lmax, den = (views[k] for k in ("kpad", "vpad", "hsum", "dlog", "lmax", "den"))
        tall = arena[:, WX:WX + J * TROWS * W]
        at = WX + J * TROWS * W
        xs = [arena[:, at + i * XS:at + (i + 1) * XS] for i in range(2)]

        stack = {k: sb(f"stack_{k}", [STACK + 2, ALL], bf16) for k in "ymx"}
        amax = sb("amax", [OM, len(CONV) + 1])
        far = sb("far", [1, 2])
        choice = sb("choice", [1, 1], i32)
        ybias = sb("ybias", [P, 1])
        distx = [sb(f"distx{i}", [P, BANK]) for i in range(2)]
        disty = [sb(f"disty{i}", [P, HW]) for i in range(2)]
        hatx = sb("hatx", [P, TAPS * HW], fp16)
        phi, plo = hatx[:, 0:TAPS * HF], hatx[:, TAPS * HF:2 * TAPS * HF]
        haty = sb("haty", [P, PAIRS * HW], fp16)
        acc = sb("acc", [C, (B + 1) * HW])
        x2seq = sb("x2seq", [C, ALL])

        ps = ctx.enter_context(nc.psum_tensor("ps", [P, 8 * BANK], fp32))

        def bank(i, n=1):
            return ps[:, i * BANK:(i + n) * BANK]

        def images(t, w=HW):
            return t[:, :].rearrange("p (j n) -> p j n", j=J)

        def padded(t):
            return t[:, :].rearrange("p (j r c) -> p j r c", j=J, r=PH)

        def shifted(t, tap):
            return padded(t)[:, :, tap // 3:tap // 3 + H, tap % 3:tap % 3 + W]

        def halfimages(ap, c):
            return grid(ap)[:, 2 * c:2 * c + 2]

        def grid(ap):
            return ap.rearrange("p (j r c) -> p j r c", j=J, r=H)

        s_x = [sem("s_x0"), sem("s_x1")]
        s_cst, s_wom, s_sel, s_rows = sem("s_cst"), sem("s_wom"), sem("s_sel"), sem("s_rows")
        s_zero = sem("s_zero")
        s_bn = sem("s_bn")
        s_kept, s_bcast = sem("s_kept"), sem("s_bcast")
        s_stats, s_pair, s_eps, s_rstd = sem("s_stats"), sem("s_pair"), sem("s_eps"), sem("s_rstd")
        s_pool, s_qkv, s_ev, s_chans = sem("s_pool"), sem("s_qkv"), sem("s_ev"), sem("s_chans")
        s_up, s_hid, s_down, s_gate = sem("s_up"), sem("s_hid"), sem("s_down"), sem("s_gate")
        s_prod, s_prodpool, s_log, s_dlog, s_exp, s_prob, s_hi, s_lo = (sem(n) for n in (
            "s_prod", "s_prodpool", "s_log", "s_dlog", "s_exp", "s_prob", "s_hi", "s_lo"))
        s_pb, s_pv, s_pbcopy, s_pvpool, s_pvsum, s_att, s_attn, s_proj = (sem(n) for n in (
            "s_pb", "s_pv", "s_pbcopy", "s_pvpool", "s_pvsum", "s_att", "s_attn", "s_proj"))
        s_dve = sem("s_dve")
        s_x2, s_x2seq = sem("s_x2"), sem("s_x2seq")
        s_tall, s_dup0, s_dup1 = sem("s_tall"), sem("s_dup0"), sem("s_dup1")
        s_conv, s_omraw, s_om, s_parts = (sem(n) for n in ("s_conv", "s_omraw", "s_om", "s_parts"))
        s_mstack = [sem(f"s_mstack{n}") for n in range(len(CONV))]
        s_stack = [sem(f"s_stack{n}") for n in range(len(CONV))]
        s_amaxed = sem("s_amaxed")
        s_amax, s_amaxT, s_choice = sem("s_amax"), sem("s_amaxT"), sem("s_choice")
        s_mb, s_maska, s_maskd = sem("s_mb"), sem("s_maska"), sem("s_maskd")
        s_staged, s_tr, s_xTa, s_xTd, s_xs, s_ybias = (sem(n) for n in (
            "s_staged", "s_tr", "s_xTa", "s_xTd", "s_xs", "s_ybias"))
        s_selx, s_sely, s_absx, s_absy, s_ux, s_uy = (sem(n) for n in (
            "s_selx", "s_sely", "s_absx", "s_absy", "s_ux", "s_uy"))
        s_cx, s_cy, s_hatx, s_haty = sem("s_cx"), sem("s_cy"), sem("s_hatx"), sem("s_haty")
        s_bx, s_by, s_hx, s_smp, s_smpfree = (sem(n) for n in ("s_bx", "s_by", "s_hx", "s_smp", "s_smpfree"))
        s_vals, s_fin, s_acc, s_y, s_out = (sem(n) for n in ("s_vals", "s_fin", "s_acc", "s_y", "s_out"))

        ONE = 1
        FROM_ONE = [s_tr, s_smpfree, s_hatx, s_haty, s_smp, s_absx, s_absy, s_hx, s_acc]

        QKV = [(t, c) for c in range(2) for t in (0, 1, 3)] + [(2, 0), (2, 1)]
        BORDER = [0, 2, 1] + list(range(3, TAPS))
        PB = [4, 6, 0]

        block = ctx.enter_context(nc.Block())

        HATS = {2: (1, 3), 3: (0, 2, 4)}
        SLICES = len(CONV) * PAIRS

        def mask_free(eng, n):
            if n >= 4:
                if n % 2 == 0:
                    eng.wait_ge(s_maska, (n - 4) // 2 + 1)
                else:
                    eng.wait_ge(s_maskd, (n - 5) // 2 + 1)

        def mask_slice(n):
            c = CONV[n // PAIRS]
            return maskb[:, n % PAIRS * ALL + c * BANK:][:, 0:BANK]

        @block.sync
        def _(sp):
            for c in range(2):
                sp.dma_start(xin[:, c * BANK:(c + 1) * BANK], x[:, c * BANK:(c + 1) * BANK]).then_inc(s_x[c], 16)
            sp.dma_start(bcast[:, :], sel16["bcast"]).then_inc(s_bcast, 16)
            sp.dma_start(womt[:, :], wom).then_inc(s_wom, 16)
            for name, n in SELS:
                sp.dma_start(sel[name][:, :].bitcast(u16), sel16[name]).then_inc(s_sel, 16)
            for k in "ymx":
                sp.dma_start(stack[k][STACK:STACK + 2, :].bitcast(u16), rows16["x" if k == "x" else "y"]).then_inc(s_rows, 16)
            sp.wait_ge(s_x2, 2)
            for h in range(HALVES):
                sp.dma_start(x2seq[:, :].rearrange("c (j h n) -> c j h n", j=J, h=HALVES)[:, :, h, :],
                             images(x2)[h * C:(h + 1) * C]).then_inc(s_x2seq, 16)
            for n, c in enumerate(CONV):
                sp.wait_ge(s_parts, n + 1)
                for row, k in enumerate("myx"):
                    for i in range(3):
                        sp.dma_start(stack[k][i * ND:(i + 1) * ND, c * BANK:(c + 1) * BANK],
                                     parts[row * ND:(row + 1) * ND, n % 2, i]).then_inc(
                                         s_mstack[n] if k == "m" else s_stack[n], 16)
            sp.wait_ge(s_y, 1)
            sp.dma_start(out, x2seq[:, :]).then_inc(s_out, 16)
            sp.wait_ge(s_out, 16)

        ZEROS = 8

        @block.gpsimd
        def _(pool):
            nc.gpsimd.memset(img[:, :], 0.0).then_inc(s_zero, 1)
            nc.gpsimd.memset(hsum[:, :], 0.0).then_inc(s_zero, 1)
            nc.gpsimd.memset(minushalf[:, :], -0.5).then_inc(s_zero, 1)
            nc.gpsimd.memset(kpad[:, :], 0.0).then_inc(s_zero, 1)
            nc.gpsimd.memset(vpad[:, :], 0.0).then_inc(s_zero, 1)
            pool.wait_ge(s_zero, 5)
            pool.wait_ge(s_eps, 1)
            nc.gpsimd.tensor_tensor(rstd[:, :], vareps[:, :], minushalf[:, :], ALU.pow).then_inc(s_rstd, 1)
            nc.gpsimd.memset(one[:, :], 1.0).then_inc(s_zero, 1)
            nc.gpsimd.memset(acc[:, :], 0.0).then_inc(s_zero, 1)
            for i in range(2):
                nc.gpsimd.memset(dup[i], 0.0).then_inc(s_zero, 1)
            for counter in FROM_ONE:
                pool.sem_inc(counter, ONE)
            for c in range(2):
                pool.wait_ge(s_ev, 2 + 3 * c)
                for t in range(TAPS - POOL_TAPS, TAPS):
                    nc.gpsimd.tensor_tensor(halfimages(prod[:, t * N:(t + 1) * N], c), halfimages(q[:, :], c),
                                            shifted(kpad, t)[:, 2 * c:2 * c + 2], ALU.mult).then_inc(s_prodpool, 1)
            pool.wait_ge(s_ev, 8)
            for t in range(2):
                pool.wait_ge(s_pbcopy, t + 1)
                nc.gpsimd.tensor_tensor(grid(prod[:, t * N:(t + 1) * N]), grid(prod[:, t * N:(t + 1) * N]),
                                        shifted(vpad, t), ALU.mult).then_inc(s_pvpool, 1)
            pool.wait_ge(s_pvpool, 2)
            nc.gpsimd.tensor_tensor(prod[:, 0:N], prod[:, 0:N], prod[:, N:2 * N], ALU.add).then_inc(s_pvpool, 1)
            pool.wait_ge(s_pvsum, 2)
            nc.gpsimd.tensor_tensor(prod[:, 2 * N:3 * N], prod[:, 2 * N:3 * N], prod[:, 4 * N:5 * N],
                                    ALU.add).then_inc(s_pvpool, 1)
            pool.wait_ge(s_x2, 2)
            nc.gpsimd.memset(tall[:, :], 0.0).then_inc(s_zero, 1)
            for i in range(2):
                nc.gpsimd.memset(xs[i][:, :], 0.0).then_inc(s_zero, 1)
            pool.wait_ge(s_zero, 12)
            nc.gpsimd.memset(vals[1][:, :], 0.0).then_inc(s_vals, 1)
            pool.wait_ge(s_eps, 2)
            nc.gpsimd.tensor_tensor(rstd[:, :], vareps[:, :], minushalf[:, :], ALU.pow).then_inc(s_rstd, 1)

            def spread(i, src_j, h, first=False):
                src = xT[:, bass.ds(src_j * (WINS * P), WINS * P)].rearrange(
                    "p (w h g c) -> p w h g c", w=WINS, h=HALVES, g=DG)[:, :, h, :, :]
                dst = xs[i][:, :].rearrange("p (w g c) -> p w g c", w=WINS, g=DG)[:, :, :, CG:2 * CG]
                if first:
                    ones = one[:, :].unsqueeze(2).unsqueeze(3).to_broadcast([P, WINS, DG, CG])
                    return nc.gpsimd.tensor_tensor(dst, src, ones, ALU.mult)
                return nc.gpsimd.tensor_copy(dst, src)

            def low_parts(p, i, n):
                t = 2 * p
                w = HW * min(2, TAPS - t)
                pool.wait_ge(s_ux, n)
                pool.wait_ge(s_haty, ONE + n - 1)
                nc.gpsimd.tensor_tensor(hatx[C:P, t * HW:t * HW + w], distx[i][C:P, 0:w],
                                        hatx[C:P, t * HW:t * HW + w], ALU.add).then_inc(s_hatx, 1)
                pool.wait_ge(s_uy, n)
                pool.wait_ge(s_hatx, ONE + n)
                nc.gpsimd.tensor_tensor(haty[C:P, p * HW:(p + 1) * HW], disty[i][C:P, :],
                                        haty[C:P, p * HW:(p + 1) * HW], ALU.add).then_inc(s_haty, 1)

            def prologue(it):
                pool.wait_ge(s_xTa, (it + 1) * 6)
                pool.wait_ge(s_xTd, (it + 1) * 6)
                spread(0, 0, 0, first=True).then_inc(s_xs, 1)
                pool.wait_ge(s_xs, it * (B + 1) + 1)
                for p in range(PAIRS - 1):
                    low_parts(p, p % 2, it * HP + p + 1)

            prologue(0)
            pool.wait_ge(s_choice, 1)
            passes = pool.value_load(choice[0:1, 0:1], min_val=1, max_val=SHIFTS)
            with pool.Fori(0, passes) as it:
                with pool.If(it > 0):
                    pool.wait_ge(s_haty, ONE + it * HP)
                    shift = nc.s_assert_within((it - 1) + it // (CENTER + 1), 0, SHIFTS - 1)
                    nc.gpsimd.tensor_copy(images(staged), images(tall)[:, :, bass.ds(shift * (WROWS * W), SROWS * W)]
                                          ).then_inc(s_staged, 1)
                    pool.wait_ge(s_smpfree, ONE + it * (UNITS * B))
                    prologue(it)
                with pool.Fori(0, J) as j:
                    for h in range(HALVES):
                        low_parts(PAIRS - 1, h, it * HP + j * (2 * PAIRS) + (h + 1) * PAIRS)
                        pool.wait_ge(s_smpfree, ONE + it * (UNITS * B) + j * (2 * UNITS) + h * UNITS)
                        pool.wait_ge(s_haty, ONE + it * HP + j * (2 * PAIRS) + (h + 1) * PAIRS)
                        spread(1 - h, j + h, 1 - h).then_inc(s_xs, 1)
                        pool.wait_ge(s_xs, it * (B + 1) + j * 2 + (h + 2))
                        for p in range(PAIRS - 1):
                            low_parts(p, (h + 1 + p) % 2, it * HP + j * (2 * PAIRS) + ((h + 1) * PAIRS + p + 1))
                low_parts(PAIRS - 1, 0, (it + 1) * HP)

        @block.scalar
        def _(act):
            act.dma_start(kept[:, :], cf[:, 0:kept.shape[1]]).then_inc(s_kept, 16)
            act.dma_start(attw, cf[:, kept.shape[1]:]).then_inc(s_cst, 16)
            act.wait_ge(s_kept, 16)
            act.wait_ge(s_zero, 5)
            for n, (t, c) in enumerate(QKV):
                dst = {0: halfimages(q[:, :], c), 1: shifted(kpad, 4)[:, 2 * c:2 * c + 2],
                       2: shifted(vpad, 4)[:, 2 * c:2 * c + 2], 3: halfimages(chans[:, :], c)}[t]
                act.wait_ge(s_qkv, n + 1)
                nc.scalar.activation(dst, bank(2 * t + c).rearrange("p (j r c) -> p j r c", j=2, r=H), ACT.Identity,
                                     bias=bias[:, t:t + 1], scale=1.0 / TAPS).then_inc(s_ev, 1)
            for c in range(2):
                act.wait_ge(s_up, c + 1)
                nc.scalar.activation(hidden[:, c * BANK:(c + 1) * BANK], bank(6 + c), ACT.Relu,
                                     bias=bias[:, 4:5]).then_inc(s_hid, 1)
            act.wait_ge(s_chans, 1)
            for c in range(2):
                act.wait_ge(s_down, c + 1)
                nc.scalar.activation(gate[:, c * BANK:(c + 1) * BANK], bank(6 + c), ACT.Tanh, bias=b2half[:, :],
                                     scale=0.5).then_inc(s_gate, 1)
            for k in range(CHUNKS):
                act.wait_ge(s_dlog, k + 1)
                e = dlog[:, k * TC * HF:(k + 1) * TC * HF]
                nc.scalar.activation(e, e, ACT.Exp, scale=SCALE).then_inc(s_exp, 1)
            for k in range(CHUNKS):
                act.wait_ge(s_prob, k + 1)
                cols = slice(k * TC * HF, (k + 1) * TC * HF)
                nc.scalar.copy(phi[:, cols], dlog[:, cols]).then_inc(s_hi, 1)
            for n in range(2):
                pos = BORDER.index(n)
                act.wait_ge(s_pb, pos + 1)
                nc.scalar.copy(prod[:, n * N:(n + 1) * N], bank(PB[pos % 3], 2)).then_inc(s_pbcopy, 1)
            act.wait_ge(s_tall, J)
            act.wait_ge(s_zero, 9)
            source = images(tall)[C:P, :, -FIRST_ROW * W:(-FIRST_ROW + H) * W].rearrange("p j (r c) -> p j r c", r=H)
            nc.scalar.copy(shifted(dup[1], 4)[0:C], source).then_inc(s_dup1, 1)
            nc.scalar.copy(shifted(dup[1], 3)[C:P], source).then_inc(s_dup1, 1)

            def offsets(n):
                act.wait_ge(s_conv, n + 1)
                if n >= 2:
                    act.wait_ge(s_amaxed, n - 1)
                o = om[:, n % 2 * BANK:(n % 2 + 1) * BANK]
                nc.scalar.activation(o, bank(4 + n % 2 * 2)[0:OM], ACT.Identity, bias=bias[0:OM, 7:8]).then_inc(s_omraw, 1)
                act.wait_ge(s_omraw, n + 1)
                nc.scalar.activation(o[0:ND], o[0:ND], ACT.Tanh, scale=0.5).then_inc(s_om, 1)

            def mask_out(n):
                act.wait_ge(s_mb, n + 1)
                nc.scalar.copy(mask_slice(n), bank(n % 4)).then_inc(s_maska, 1)

            def evac(slot, n, bank_, w, waits_smp):
                act.wait_ge(s_bx, n)
                act.wait_ge(s_smp, ONE + waits_smp)
                nc.scalar.copy(hx[:, slot * BANK:slot * BANK + w], bank(bank_)[:, 0:w]).then_inc(s_hx, 1)

            def distance_x(p, i, n, free):
                w = HW * min(2, TAPS - 2 * p)
                act.wait_ge(s_selx, n)
                act.wait_ge(s_hatx, ONE + free)
                nc.scalar.activation(distx[i][:, 0:w], bank(5)[:, 0:w], ACT.Abs).then_inc(s_absx, 1)

            def distance_y(p, i, n, free):
                act.wait_ge(s_sely, n)
                act.wait_ge(s_haty, ONE + free)
                nc.scalar.activation(disty[i][:, :], bank(7)[:, 0:HW], ACT.Abs, bias=ybias[:, :]).then_inc(s_absy, 1)

            def hat_x(p, i, n):
                t = 2 * p
                w = HW * min(2, TAPS - t)
                act.wait_ge(s_absx, ONE + n)
                nc.scalar.activation(hatx[:, t * HW:t * HW + w], distx[i][:, 0:w], ACT.Relu, bias=1.0,
                                     scale=-1.0).then_inc(s_cx, 1)

            def hat_y(p, i, n):
                act.wait_ge(s_absy, ONE + n)
                nc.scalar.activation(haty[:, p * HW:(p + 1) * HW], disty[i][:, :], ACT.Relu, bias=1.0,
                                     scale=-1.0).then_inc(s_cy, 1)

            def windows_out(it):
                for g in range(0, 12, 2):
                    act.wait_ge(s_tr, ONE + it * 12 + (g + 1))
                    nc.scalar.copy(xT[:, g * BANK:(g + 1) * BANK], bank(g % 4)).then_inc(s_xTa, 1)

            def hats(p, it):
                n = it * HP + p + 1
                free = it * HP + max(p - 1, 0)
                distance_x(p, p % 2, n, free)
                distance_y(p, p % 2, n, free)
                hat_x(p, p % 2, n)
                hat_y(p, p % 2, n)

            offsets(0)
            windows_out(0)
            offsets(1)
            act.wait_ge(s_ybias, 1)
            hat = 0
            for step in (2, 3):
                for p in range(PAIRS):
                    if p in HATS[step]:
                        hats(hat, 0)
                        hat += 1
                    if ((step - 2) * PAIRS + p) % 2 == 0:
                        mask_out((step - 2) * PAIRS + p)
                offsets(step)
            for n in range(2 * PAIRS, SLICES, 2):
                mask_out(n)
            for g in range(AHEAD_X):
                evac(g, g + 1, g % 2, BANK, 0)
            act.wait_ge(s_choice, 1)
            passes = act.value_load(choice[0:1, 0:1], min_val=1, max_val=SHIFTS)
            with act.Fori(0, passes) as it:
                with act.If(it > 0):
                    windows_out(it)
                    act.wait_ge(s_ybias, it + 1)
                    for p in range(PAIRS):
                        hats(p, it)
                        if p == 0:
                            for g in range(AHEAD_X):
                                evac(g, it * UPX + g + 1, g % 2, BANK, it * UP)
                with act.Fori(0, J) as j:
                    for h in range(HALVES):
                        for u in range(UNITS):
                            g = h * UNITS + u + AHEAD_X
                            p = (u + AHEAD_X) % UNITS // DG
                            evac(g % 4, it * UPX + j * (2 * UNITS) + g + 1, g % 2, HW * min(2, TAPS - 2 * p),
                                 it * UP + j * (2 * UNITS) + g - 3)
                            n = it * HP + j * (2 * PAIRS) + ((h + 1) * PAIRS + u // 4 + 1)
                            i = (h + 1 + u // 4) % 2
                            if u % 4 == 2:
                                distance_x(u // 4, i, n, n - 2)
                                distance_y(u // 4, i, n, n - 2)
                            if u % 4 == 3:
                                hat_x(u // 4, i, n)
                                hat_y(u // 4, i, n)

        @block.vector
        def _(dve):
            chain = [0]

            def link(ins):
                chain[0] += 1
                ins.then_inc(s_dve, 1)
                dve.wait_ge(s_dve, chain[0])

            def norm_stats(src, j):
                for i in (j, j + 1):
                    nc.vector.bn_stats(halfstat[:, 6 * i:6 * i + 6], src[:, i * HW:(i + 1) * HW]).then_inc(s_bn, 1)
                n = bn[0] = bn[0] + 2
                dve.wait_ge(s_bn, n)
                for i in (j, j + 1):
                    nc.vector.bn_aggr(meanvar[:, 2 * i:2 * i + 2], halfstat[:, 6 * i:6 * i + 6]).then_inc(s_stats, 1)

            def norm(src, n):
                dve.wait_ge(s_pair, n)
                link(nc.vector.tensor_copy(pair[:, :], bank(7)[:, 0:4 * J]))
                gap = pair[:, 2 * J:4 * J].rearrange("p (j s) -> p j s", s=2)[:, :, 0]
                var = pair[:, 0:2 * J].rearrange("p (j s) -> p j s", s=2)[:, :, 1]
                link(nc.vector.tensor_tensor(gap2[:, :], gap, gap, ALU.mult))
                nc.vector.scalar_tensor_tensor(vareps[:, :], gap2[:, :], EPS, var, ALU.add, ALU.add).then_inc(s_eps, 1)
                dve.wait_ge(s_rstd, n)

            def normalise(dst, src, j, rows=slice(0, P)):
                return nc.vector.tensor_scalar(dst, grid(src[:, :])[rows, j], pair[rows, 2 * j:2 * j + 1],
                                               rstd[rows, j:j + 1], ALU.subtract, ALU.mult)

            bn = [0]
            for c in range(2):
                dve.wait_ge(s_x[c], 16)
                norm_stats(xin, 2 * c)
            dve.wait_ge(s_zero, 2)
            norm(xin, 1)
            for j in range(J):
                ins = normalise(shifted(img, 4)[:, j], xin, j)
            link(ins)
            for c in range(2):
                im = padded(img)[:, 2 * c:2 * c + 2]
                hs = hsum[:, :].rearrange("p (j r c) -> p j r c", j=J, r=PH)[:, 2 * c:2 * c + 2]
                mid = hs[:, :, 1:H + 1, :]
                po = halfimages(pooled[:, :], c)
                link(nc.vector.tensor_tensor(mid, im[:, :, 1:H + 1, 0:W], im[:, :, 1:H + 1, 1:W + 1], ALU.add))
                link(nc.vector.tensor_tensor(mid, mid, im[:, :, 1:H + 1, 2:W + 2], ALU.add))
                link(nc.vector.tensor_tensor(po, hs[:, :, 0:H, :], hs[:, :, 1:H + 1, :], ALU.add))
                nc.vector.tensor_tensor(po, po, hs[:, :, 2:H + 2, :], ALU.add).then_inc(s_pool, 1)
            dve.wait_ge(s_kept, 16)
            nc.vector.tensor_scalar(b2half[:, :], bias[:, 5:6], 0.5, None, ALU.mult).then_inc(s_chans, 1)
            for c in range(2):
                dve.wait_ge(s_ev, 2 + 3 * c)
                for t in range(TAPS - POOL_TAPS):
                    nc.vector.tensor_tensor(halfimages(prod[:, t * N:(t + 1) * N], c), halfimages(q[:, :], c),
                                            shifted(kpad, t)[:, 2 * c:2 * c + 2], ALU.mult).then_inc(s_prod, 1)
            dve.wait_ge(s_gate, 2)
            link(nc.vector.tensor_scalar(gate[:, :], gate[:, :], 0.5, 1.5, ALU.mult, ALU.add))
            dve.wait_ge(s_log, 2 * TAPS)
            logits = ps[:, 0:TAPS * HF].rearrange("p (t n) -> p t n", t=TAPS)
            d3 = dlog[:, :].rearrange("p (t n) -> p t n", t=TAPS)
            link(nc.vector.tensor_reduce(lmax[:, :], logits.rearrange("p t n -> p n t"), AX.X, ALU.max))
            for k in range(CHUNKS):
                taps = slice(k * TC, (k + 1) * TC)
                nc.vector.tensor_tensor(d3[:, taps], logits[:, taps], lmax[:, :].unsqueeze(1).to_broadcast([P, TC, HF]),
                                        ALU.subtract).then_inc(s_dlog, 1)
            dve.wait_ge(s_exp, CHUNKS)
            link(nc.vector.tensor_reduce(den[:, :], d3.rearrange("p t n -> p n t"), AX.X, ALU.add))
            link(nc.vector.reciprocal(den[:, :], den[:, :]))
            for k in range(CHUNKS):
                taps = slice(k * TC, (k + 1) * TC)
                nc.vector.tensor_tensor(d3[:, taps], d3[:, taps], den[:, :].unsqueeze(1).to_broadcast([P, TC, HF]),
                                        ALU.mult).then_inc(s_prob, 1)
            for k in range(CHUNKS):
                dve.wait_ge(s_hi, k + 1)
                cols = slice(k * TC * HF, (k + 1) * TC * HF)
                dve.wait_ge(s_prob, k + 1)
                nc.vector.tensor_tensor(plo[:, cols], dlog[:, cols], phi[:, cols], ALU.subtract).then_inc(s_lo, 1)
            dve.wait_ge(s_ev, 8)

            def pv_sum(a, b, n):
                dve.wait_ge(s_pv, n)
                nc.vector.tensor_tensor(prod[:, a * N:(a + 1) * N], prod[:, a * N:(a + 1) * N],
                                        prod[:, b * N:(b + 1) * N], ALU.add).then_inc(s_pvsum, 1)

            for t in range(2, TAPS):
                pos = BORDER.index(t)
                dve.wait_ge(s_pb, pos + 1)
                nc.vector.tensor_tensor(grid(prod[:, t * N:(t + 1) * N]), grid(bank(PB[pos % 3], 2)),
                                        shifted(vpad, t), ALU.mult).then_inc(s_pv, 1)
                if t % 2 == 0 and t > 2:
                    pv_sum(t - 2, t - 1, t - 2)
            for c in range(2):
                dve.wait_ge(s_att, c + 1)
                cols = slice(c * BANK, (c + 1) * BANK)
                nc.vector.tensor_tensor(att[:, cols], bank(2 + c), gate[:, cols], ALU.mult).then_inc(s_attn, 1)
            for c in range(2):
                cols = slice(c * BANK, (c + 1) * BANK)
                dve.wait_ge(s_proj, c + 1)
                nc.vector.scalar_tensor_tensor(x2[:, cols], bank(c), bias[:, 6:7], xin[:, cols], ALU.add,
                                               ALU.add).then_inc(s_x2, 1)
            for c in range(2):
                dve.wait_ge(s_x2, c + 1)
                norm_stats(x2, 2 * c)
            norm(x2, 2)
            dve.wait_ge(s_zero, 10)
            low = slice(0, C)
            for part in range(2):
                for j in (2 * part, 2 * part + 1):
                    normalise(shifted(dup[0], 4)[low, j], x2, j, low)
                    ins = normalise(shifted(dup[0], 3)[C:P, j], x2, j, low)
                ins.then_inc(s_dup0, 1)
                if part == 0:
                    for j in range(J):
                        normalise(tall[:, :].rearrange("p (j r c) -> p j r c", j=J, r=TROWS)[
                            :, j, -FIRST_ROW:-FIRST_ROW + H, :], x2, j).then_inc(s_tall, 1)
            dve.wait_ge(s_x2seq, 16 * HALVES)
            dve.wait_ge(s_dup0, 2)

            def offset_parts(n):
                dve.wait_ge(s_om, n + 1)
                if n >= 2:
                    dve.wait_ge(s_mstack[n - 2], 16 * 3)
                    dve.wait_ge(s_stack[n - 2], 16 * 6)
                o = om[:, n % 2 * BANK:(n % 2 + 1) * BANK]
                part = [parts[:, n % 2, i] for i in range(3)]
                link(nc.vector.tensor_copy(part[0], o))
                link(nc.vector.tensor_tensor(rest, o, part[0], ALU.subtract))
                link(nc.vector.tensor_copy(part[1], rest))
                nc.vector.tensor_tensor(part[2], rest, part[1], ALU.subtract).then_inc(s_parts, 1)
                nc.vector.tensor_reduce(amax[:, n:n + 1], o, AX.X, ALU.max,
                                        apply_absolute_value=True).then_inc(s_amaxed, 1)

            def mask_out(n):
                dve.wait_ge(s_mb, n + 1)
                nc.vector.tensor_copy(mask_slice(n), bank(n % 4)).then_inc(s_maskd, 1)

            def exact_x(p, i, n):
                w = HW * min(2, TAPS - 2 * p)
                dve.wait_ge(s_cx, n)
                nc.vector.tensor_scalar(distx[i][:, 0:w], distx[i][:, 0:w], 1.0, 1.0, ALU.min,
                                        ALU.subtract).then_inc(s_ux, 1)

            def exact_y(p, i, n):
                dve.wait_ge(s_cy, n)
                nc.vector.tensor_scalar(disty[i][:, :], disty[i][:, :], 1.0, 1.0, ALU.min,
                                        ALU.subtract).then_inc(s_uy, 1)

            def sample(g, w, n, nx, nfree):
                s = g % 4
                dve.wait_ge(s_by, n)
                dve.wait_ge(s_hx, ONE + nx)
                dve.wait_ge(s_smpfree, ONE + nfree)
                nc.vector.tensor_tensor(smp[:, s * BANK:s * BANK + w], bank(2 + g % 2)[:, 0:w],
                                        hx[:, s * BANK:s * BANK + w], ALU.mult).then_inc(s_smp, 1)

            def accumulate(slot, n):
                dve.wait_ge(s_fin, n)
                dve.wait_ge(s_acc, ONE + n - 1)
                a = acc[:, bass.ds(slot * HW, HW)]
                nc.vector.tensor_tensor(a, bank(7)[0:C, 0:HW], a, ALU.add).then_inc(s_acc, 1)

            def windows_out(it):
                for g in range(1, 12, 2):
                    dve.wait_ge(s_tr, ONE + it * 12 + (g + 1))
                    nc.vector.tensor_copy(xT[:, g * BANK:(g + 1) * BANK], bank(g % 4)).then_inc(s_xTd, 1)

            offset_parts(0)
            nc.vector.tensor_copy(ybias[:, :], table[:, 0:1]).then_inc(s_ybias, 1)
            windows_out(0)
            offset_parts(1)
            for step in (2, 3):
                for p in range(PAIRS):
                    if ((step - 2) * PAIRS + p) % 2:
                        mask_out((step - 2) * PAIRS + p)
                for p in range(len(HATS[2])) if step == 2 else range(len(HATS[2]), PAIRS - 1):
                    exact_x(p, p % 2, p + 1)
                    exact_y(p, p % 2, p + 1)
                offset_parts(step)
            dve.wait_ge(s_amaxed, len(CONV))
            nc.vector.tensor_reduce(amax[:, len(CONV):], amax[:, 0:len(CONV)], AX.X, ALU.max).then_inc(s_amax, 1)
            dve.wait_ge(s_amaxT, 1)
            link(nc.vector.tensor_reduce(far[0:1, 0:1], bank(6)[0:1, 0:OM], AX.X, ALU.max))
            link(nc.vector.tensor_scalar(far[0:1, 1:2], far[0:1, 0:1], float(REACH), float(SHIFTS - 1), ALU.is_gt,
                                         ALU.mult))
            nc.vector.tensor_scalar(choice[0:1, 0:1], far[0:1, 1:2], 1.0, None, ALU.add).then_inc(s_choice, 1)
            for n in range(2 * PAIRS + 1, SLICES, 2):
                mask_out(n)
            for n in range(len(CONV)):
                dve.wait_ge(s_stack[n], 16 * 6)
            for g in range(AHEAD):
                sample(g, BANK, g + 1, g + 1, 0)
            dve.wait_ge(s_choice, 1)
            passes = dve.value_load(choice[0:1, 0:1], min_val=1, max_val=SHIFTS)
            dve.wait_ge(s_maska, SLICES // 2)
            with dve.Fori(0, passes) as it:
                with dve.If(it > 0):
                    dve.wait_ge(s_absy, ONE + it * HP)
                    nc.vector.tensor_copy(ybias[:, :], table[:, bass.ds(nc.s_assert_within(it, 0, SHIFTS - 1), 1)]
                                          ).then_inc(s_ybias, 1)
                    windows_out(it)
                    for p in range(PAIRS - 1):
                        exact_x(p, p % 2, it * HP + p + 1)
                        exact_y(p, p % 2, it * HP + p + 1)
                    for g in range(AHEAD):
                        sample(g, BANK, it * UP + g + 1, it * UPX + g + 1, it * (UNITS * B))
                with dve.Fori(0, J) as j:
                    for h in range(HALVES):
                        for u in range(UNITS):
                            if u == 6:
                                accumulate(j * 2 + h, it * (B + 1) + j * 2 + (h + 1))
                            g = h * UNITS + u + AHEAD
                            p = (u + AHEAD) % UNITS // DG
                            sample(g, HW * min(2, TAPS - 2 * p), it * UP + j * (2 * UNITS) + g + 1,
                                   it * UPX + j * (2 * UNITS) + g + 1,
                                   it * (UNITS * B) + j * (2 * UNITS) + max(g - 3, 0))
                            n = it * HP + j * (2 * PAIRS) + ((h + 1) * PAIRS + u // 4)
                            if u % 4 == 0:
                                exact_x((u // 4 - 1) % PAIRS, (h + u // 4) % 2, n)
                            if u % 4 == 1:
                                exact_y((u // 4 - 1) % PAIRS, (h + u // 4) % 2, n)
                            if u % 4 == 3:
                                p = u // 4
                                dve.wait_ge(s_smpfree, ONE + it * (UNITS * B) + j * (2 * UNITS) + (h * UNITS + u + 1))
                                nc.vector.tensor_tensor(
                                    vals[h][:, p * HW:(p + 1) * HW], bank(4 + 2 * ((h + p) % 2))[:, 0:HW],
                                    maskb[:, bass.ds(j * HW + (p * ALL + h * N), HW)], ALU.mult).then_inc(s_vals, 1)
                exact_x(PAIRS - 1, 0, (it + 1) * HP)
                exact_y(PAIRS - 1, 0, (it + 1) * HP)
                accumulate(B, it * (B + 1) + (B + 1))
            dve.wait_ge(s_acc, ONE + passes * (B + 1))
            nc.vector.scalar_tensor_tensor(x2seq[:, :], acc[:, HW:], 0.0, x2seq[:, :], ALU.max, ALU.add).then_inc(s_y, 1)

        @block.tensor
        def _(pe):
            def pair_stats(n):
                pe.wait_ge(s_stats, n * J)
                nc.tensor.matmul(bank(7)[:, 0:2 * J], gnp, meanvar[:, :], start=True, stop=True)
                nc.tensor.matmul(bank(7)[:, 2 * J:4 * J], gnd, meanvar[:, :], start=True, stop=True).then_inc(s_pair, 1)

            def dense(dst, w, src, c, signal):
                nc.tensor.matmul(bank(dst + c), w, src[:, c * BANK:(c + 1) * BANK], start=True, stop=True).then_inc(signal, 1)

            pe.wait_ge(s_kept, 16)
            pair_stats(1)
            pe.wait_ge(s_cst, 16)
            for t, c in QKV:
                pe.wait_ge(s_pool, c + 1)
                dense(2 * t, cst["wqkv"][:, t * P:(t + 1) * P], pooled, c, s_qkv)
            for c in range(2):
                pe.wait_ge(s_ev, 3 + 3 * c)
                dense(6, cst["w1"], chans, c, s_up)

            def logits(t, c, n):
                if t < TAPS - POOL_TAPS:
                    pe.wait_ge(s_prod, n)
                else:
                    pe.wait_ge(s_prodpool, n)
                for part in range(2):
                    for j in (2 * c, 2 * c + 1):
                        ins = nc.tensor.matmul(ps[32 * j:32 * j + 32, t * HF:(t + 1) * HF],
                                               cst["headsum"][:, 32 * part:32 * part + 32],
                                               prod[:, t * N + j * HW + part * HF:][:, 0:HF], start=(part == 0),
                                               stop=(part == 1), skip_group_check=True)
                ins.then_inc(s_log, 1)

            mine = TAPS - POOL_TAPS
            for c in range(2):
                for k in range(POOL_TAPS):
                    logits(2 * k, c, c * mine + 2 * k + 1)
                    logits(2 * k + 1, c, c * mine + 2 * k + 2)
                    if c == 0 and k == 0:
                        for i in range(2):
                            pe.wait_ge(s_hid, i + 1)
                            dense(6, cst["w2"], hidden, i, s_down)
                    logits(mine + k, c, c * POOL_TAPS + k + 1)
            pe.wait_ge(s_gate, 2)
            pe.wait_ge(s_bcast, 16)
            for pos, t in enumerate(BORDER):
                pe.wait_ge(s_lo, t // TC + 1)
                if pos >= 3:
                    before = BORDER[pos - 3]
                    if before < 2:
                        pe.wait_ge(s_pbcopy, before + 1)
                    else:
                        pe.wait_ge(s_pv, before - 1)
                for i in range(2 * J):
                    c = (3 * DG + i) * P
                    for prob in (phi, plo):
                        ins = nc.tensor.matmul(ps[:, PB[pos % 3] * BANK + i * HF:][:, 0:HF], bcast[:, c:c + P],
                                               prob[:, t * HF:(t + 1) * HF], start=(prob is phi), stop=(prob is plo))
                ins.then_inc(s_pb, 1)
            for n, (t, signal, count) in enumerate([(0, s_pvpool, 3), (6, s_pvsum, 3), (2, s_pvpool, 4), (8, s_pv, 7)]):
                pe.wait_ge(signal, count)
                for c in range(2):
                    ins = nc.tensor.matmul(bank(2 + c), ident, prod[:, t * N + c * BANK:][:, 0:BANK],
                                           start=(n == 0), stop=(n == 3))
                    if n == 3:
                        ins.then_inc(s_att, 1)
            for c in range(2):
                pe.wait_ge(s_attn, c + 1)
                dense(0, cst["wp"], att, c, s_proj)
            pair_stats(2)
            def select(p, image, n, nacc):
                cols = bass.ds(image * HW, HW)
                pe.wait_ge(s_absx, ONE + n - 1)
                for t in range(2 * p, min(2 * p + 2, TAPS)):
                    ins = nc.tensor.matmul(bank(5)[:, t % 2 * HW:(t % 2 + 1) * HW], sel["selx"][:, t * P:(t + 1) * P],
                                           stack["x"][:, cols], start=True, stop=True)
                ins.then_inc(s_selx, 1)
                pe.wait_ge(s_absy, ONE + n - 1)
                pe.wait_ge(s_acc, ONE + nacc)
                nc.tensor.matmul(bank(7)[:, 0:HW], sel["sely"][:, p * P:(p + 1) * P], stack["y"][:, cols],
                                 start=True, stop=True).then_inc(s_sely, 1)

            def issue_x(g, unit, nhat, n):
                p, d = unit // DG, unit % DG
                taps = min(2, TAPS - 2 * p)
                if d == 0:
                    pe.wait_ge(s_hatx, ONE + nhat)
                pe.wait_ge(s_hx, ONE + n)
                nc.tensor.matmul(bank(g % 2)[:, 0:taps * HW], bcast[:, d * P:(d + 1) * P],
                                 hatx[:, 2 * p * HW:(2 * p + taps) * HW], start=True, stop=True).then_inc(s_bx, 1)

            def issue_y(g, unit, nhat, n):
                p, d = unit // DG, unit % DG
                taps = min(2, TAPS - 2 * p)
                if d == 0:
                    pe.wait_ge(s_haty, ONE + nhat)
                pe.wait_ge(s_smp, ONE + n)
                for a in range(taps):
                    at = (DG + 2 * d + a) * P
                    ins = nc.tensor.matmul(bank(2 + g % 2)[:, a * HW:(a + 1) * HW], bcast[:, at:at + P],
                                           haty[:, p * HW:(p + 1) * HW], start=True, stop=True)
                ins.then_inc(s_by, 1)

            def products(h, u, n, nv):
                p, d0 = u // DG, u % DG
                taps = min(2, TAPS - 2 * p)
                if d0 == 0:
                    pe.wait_ge(s_vals, nv)
                pe.wait_ge(s_smp, ONE + n)
                slot = bank(4 + 2 * ((h + p) % 2))
                for a in range(taps):
                    for s in range(STRIPS):
                        for d in (d0, d0 + 1):
                            w = ((s * 3 + (2 * p + a) // 3) * DG + d) * XSW + (CG if a == 0 else 0)
                            o = s * STRIP * W
                            m = (h * UNITS + u + d - d0) % 4 * BANK + a * HW + s * STRIP * W
                            ins = nc.tensor.matmul(slot[32 * d:32 * d + 32, o:o + STRIP * W], xs[h][:, w:w + 2 * CG],
                                                   smp[:, m:m + STRIP * W], start=(a == 0 and s == 0),
                                                   stop=(a == taps - 1), skip_group_check=True)
                ins.then_inc(s_smpfree, 2)

            def final(i, pairs, n, nv, ny):
                if pairs[0] == 0:
                    pe.wait_ge(s_vals, nv)
                    pe.wait_ge(s_absy, ONE + ny)
                    pe.wait_ge(s_acc, ONE + n - 1)
                for p in pairs:
                    ins = nc.tensor.matmul(bank(7)[0:C, 0:HW], cst["wfin"][:, p * C:(p + 1) * C],
                                           vals[i][:, p * HW:(p + 1) * HW], start=(p == 0), stop=(p == PAIRS - 1))
                if pairs[-1] == PAIRS - 1:
                    ins.then_inc(s_fin, 1)

            def windows(g, it, src, first_row):
                if g >= 4:
                    if g % 2 == 0:
                        pe.wait_ge(s_xTa, it * 6 + (g - 4) // 2 + 1)
                    else:
                        pe.wait_ge(s_xTd, it * 6 + (g - 5) // 2 + 1)
                for k in range(4):
                    j, w = divmod(4 * g + k, WINS)
                    row = first_row + w // 3 * STRIP + w % 3
                    ins = nc.tensor.transpose(bank(g % 4)[:, k * P:(k + 1) * P],
                                              images(src)[:, j, row * W:(row + WROWS) * W], ident)
                ins.then_inc(s_tr, 1)

            def convolve(n, k):
                h, j = CONV[n] // 2, CONV[n] % 2 * 2
                ky, single = divmod(k, 2)
                if k == 0:
                    if h == 0:
                        pe.wait_ge(s_dup0, CONV[n] + 1)
                    else:
                        pe.wait_ge(s_dup1, 2)
                    if n >= 2:
                        pe.wait_ge(s_omraw, n - 1)
                ins = nc.tensor.matmul(bank(4 + n % 2 * 2)[0:OM], womt[:, k * OM:(k + 1) * OM],
                                       shifted(dup[h], 3 * ky + 2 * single)[:, j:j + 2], start=(k == 0),
                                       stop=(k == TAPSTEPS - 1))
                if k == TAPSTEPS - 1:
                    ins.then_inc(s_conv, 1)

            def spread_mask(n):
                c, p = CONV[n // PAIRS], n % PAIRS
                if p == 0:
                    pe.wait_ge(s_mstack[n // PAIRS], 16 * 3)
                mask_free(pe, n)
                nc.tensor.matmul(bank(n % 4), sel["selm"][:, p * P:(p + 1) * P], stack["m"][:, c * BANK:(c + 1) * BANK],
                                 start=True, stop=True).then_inc(s_mb, 1)

            pe.wait_ge(s_wom, 16)
            for k in range(TAPSTEPS):
                convolve(0, k)
            pe.wait_ge(s_tall, J)
            for k in range(TAPSTEPS):
                convolve(1, k)
                windows(2 * k, 0, tall, WROWS * CENTER)
                windows(2 * k + 1, 0, tall, WROWS * CENTER)
            pe.wait_ge(s_xTa, 6)
            pe.wait_ge(s_xTd, 6)
            pe.wait_ge(s_rows, 16 * 3)
            pe.wait_ge(s_sel, 16 * len(SELS))
            pe.wait_ge(s_stack[0], 16 * 6)
            hat = 0
            for n in (2, 3):
                for k in range(TAPSTEPS):
                    convolve(n, k)
                    if k < PAIRS:
                        if k in HATS[n]:
                            select(hat, 0, hat + 1, 0)
                            hat += 1
                        spread_mask((n - 2) * PAIRS + k)
            pe.wait_ge(s_amax, 1)
            nc.tensor.matmul(bank(6)[0:1, 0:OM], amax[:, len(CONV):], ident[0:OM, 0:OM], start=True, stop=True).then_inc(s_amaxT, 1)
            for n in range(2 * PAIRS, SLICES):
                spread_mask(n)
            pe.wait_ge(s_maska, SLICES // 2)
            pe.wait_ge(s_maskd, SLICES // 2)
            for g in range(AHEAD_X):
                issue_x(g, g, 1, max(g - 1, 0))
            for g in range(AHEAD):
                issue_y(g, g, 1, 0)
            for n in range(1, len(CONV)):
                pe.wait_ge(s_stack[n], 16 * 6)
            pe.wait_ge(s_choice, 1)
            passes = pe.value_load(choice[0:1, 0:1], min_val=1, max_val=SHIFTS)

            with pe.Fori(0, passes) as it:
                with pe.If(it > 0):
                    pe.wait_ge(s_staged, it)
                    pe.wait_ge(s_smp, ONE + it * UP)
                    pe.wait_ge(s_hx, ONE + it * UPX)
                    for g in range(12):
                        windows(g, it, staged, 0)
                    pe.wait_ge(s_xTa, (it + 1) * 6)
                    pe.wait_ge(s_xTd, (it + 1) * 6)
                    for p in range(PAIRS):
                        select(p, 0, it * HP + p + 1, it * (B + 1))
                        if p == 0:
                            for g in range(AHEAD_X):
                                issue_x(g, g, it * HP + 1, it * UPX + max(g - 1, 0))
                    for g in range(AHEAD):
                        issue_y(g, g, it * HP + 1, it * UP)
                with pe.Fori(0, J) as j:
                    for h in range(HALVES):
                        pe.wait_ge(s_xs, it * (B + 1) + j * 2 + (h + 1))
                        for u in range(UNITS):
                            g = h * UNITS + u
                            nxt, unit = divmod(u + AHEAD, UNITS)
                            issue_y(g + AHEAD, unit, it * HP + j * (2 * PAIRS) + ((h + nxt) * PAIRS + unit // DG + 1),
                                    it * UP + j * (2 * UNITS) + (g + AHEAD - 1))
                            if u % 2:
                                products(h, u - 1, it * UP + j * (2 * UNITS) + (g + 1),
                                         it * (PAIRS * B) + j * (2 * PAIRS) + (h * PAIRS + u // DG))
                            nxt, unit = divmod(u + AHEAD_X, UNITS)
                            issue_x(g + AHEAD_X, unit, it * HP + j * (2 * PAIRS) + ((h + nxt) * PAIRS + unit // DG + 1),
                                    it * UPX + j * (2 * UNITS) + (g + AHEAD_X - 1))
                            if 3 <= u <= 5:
                                final(1 - h, [(0,), (1, 2), (3, 4)][u - 3], it * (B + 1) + j * 2 + (h + 1),
                                      it * (PAIRS * B) + j * (2 * PAIRS) + (h * PAIRS + 1),
                                      it * HP + j * (2 * PAIRS) + ((h + 1) * PAIRS + 1))
                            if u % 4 == 2:
                                select(u // 4, j + (J if h == 0 else 1),
                                       it * HP + j * (2 * PAIRS) + ((h + 1) * PAIRS + u // 4 + 1),
                                       it * (B + 1) + j * 2 + (h + (u > 4)))
                final(1, range(PAIRS), it * (B + 1) + (B + 1), it * (PAIRS * B) + (PAIRS * B + 1), (it + 1) * HP)


def _layout(a):
    import numpy as np

    def diag(w):
        o = np.zeros((HALVES * w.shape[0], HALVES * w.shape[1]), np.float32)
        for h in range(HALVES):
            o[h * w.shape[0]:(h + 1) * w.shape[0], h * w.shape[1]:(h + 1) * w.shape[1]] = w
        return np.pad(o, ((0, P - o.shape[0]), (0, P - o.shape[1])))

    def rows(v):
        v = np.concatenate([v] * HALVES)
        return np.pad(v, (0, P - v.shape[0]))

    i = np.arange(P)
    gnp = np.where(i[:, None] // GC == i[None] // GC, 1.0 / GC, 0.0)
    wq = a["L0_conv_W_qkv"].reshape(C, 4, C)
    headsum = np.zeros((P, 2, 2, HALVES * HEADS))
    spread = np.zeros((J, 2, HALVES * HEADS, J, 2, P))
    for p in range(P):
        for part in range(2):
            headsum[p, part, part, p // HD] = 1
            for j in range(J):
                spread[j, part, p // HD, j, part, p] = 1
    wd = a["L1_conv_w_dcn"].reshape(C, DG, CG, TAPS)
    wfin = np.zeros((DG, 2, CG, PAIRS, C), np.float32)
    for t in range(TAPS):
        wfin[:, t % 2, :, t // 2, :] = wd[:, :, :, t].transpose(1, 2, 0)
    order = [2 * ND + n for n in range(ND)] + [2 * n for n in range(ND)] + [2 * n + 1 for n in range(ND)]
    wo = a["L1_conv_w_om"][order].reshape(OM, C, TAPS).transpose(1, 2, 0)
    wom = np.zeros((2, C, 3, 2, OM), np.float32)
    for ky in range(3):
        wom[0, :, ky, 0], wom[1, :, ky, 0], wom[0, :, ky, 1] = (wo[:, 3 * ky + kx] for kx in range(3))
    bq = a["L0_conv_b_qkv"].reshape(C, 4)
    bias = np.stack([rows(bq[:, t]) for t in range(4)] + [
        rows(a["L0_conv_b1"]), rows(a["L0_conv_b2"]), rows(a["L0_conv_bp"]),
        np.pad(a["L1_conv_b_om"][order], (0, P - OM))], axis=1)
    table = np.tile([-float(WROWS) * (s - CENTER) for s in (2, 0, 1, 3, 4)], (P, 1))
    cf = np.concatenate([gnp, np.eye(P) - gnp, np.eye(P), wfin.reshape(P, -1), bias, table] + [
        diag(wq[:, t].T) for t in range(4)] + [diag(a["L0_conv_W1"].T), diag(a["L0_conv_W2"].T),
                                               diag(a["L0_conv_Wp"].T), headsum.reshape(P, -1)], axis=1).astype(np.float32)

    sely, selx, selm = (np.zeros((STACK + 2, n, P), np.float32) for n in (PAIRS, TAPS, PAIRS))
    for t in range(TAPS):
        p, ab = divmod(t, 2)
        for d in range(DG):
            src = [i * ND + d * TAPS + t for i in range(3)]
            for part in range(2):
                for r in range(WROWS):
                    c = part * 64 + ab * 32 + d * WROWS + r
                    sely[src, p, c] = 1
                    sely[STACK, p, c] = 1
                    sely[STACK + 1, p, c] = -r
                for x in range(W):
                    c = part * 64 + d * W + x
                    selx[src, t, c] = 1
                    selx[STACK, t, c] = 1
                    selx[STACK + 1, t, c] = t % 3 - 1 - x
            c = slice(d * 32 + ab * CG, d * 32 + ab * CG + CG)
            selm[src, p, c] = 0.5
            selm[STACK + 1, p, c] = 0.5
    bx, by = np.zeros((P, DG, P)), np.zeros((P, DG, 2, P))
    for d in range(DG):
        for part in range(2):
            for m in range(P):
                bx[part * 64 + d * W + m % W, d, m] = 1 - 2 * part
                for ab in range(2):
                    by[part * 64 + ab * 32 + d * WROWS + m // W, d, ab, m] = 1 - 2 * part
    n = np.arange(ALL) % HW
    f16 = np.float16

    def bf16_bits(v):
        return (v.astype(np.float32).view(np.uint32) >> 16).astype(np.uint16)

    return {
        "x": a["x"].reshape(HALVES, J, C, HW).transpose(0, 2, 1, 3).reshape(P, N), "cf": cf,
        "wom": wom.reshape(P, -1),
        "bcast": np.concatenate([bx.reshape(P, -1), by.reshape(P, -1), spread.reshape(P, -1)], 1).astype(f16),
        "sely": bf16_bits(sely.reshape(STACK + 2, -1)), "selx": bf16_bits(selx.reshape(STACK + 2, -1)),
        "selm": bf16_bits(selm.reshape(STACK + 2, -1)),
        "rowsy": bf16_bits(np.stack([n // W % STRIP + REACH, np.ones(ALL)])),
        "rowsx": bf16_bits(np.stack([n % W, np.ones(ALL)])),
    }


def kernel(**inputs):
    import numpy as np
    import concourse.bacc as bacc
    from concourse.bass_utils import run_bass_kernel_spmd as run

    arrays = {k: np.ascontiguousarray(v) for k, v in _layout({k: np.asarray(v) for k, v in inputs.items()}).items()}
    nc = bacc.Bacc("TRN2", target_bir_lowering=False, num_devices=1)
    d = {k: nc.dram_tensor("in_" + k, v.shape, mybir.dt.from_np(v.dtype), kind="ExternalInput").ap() for k, v in arrays.items()}
    out = nc.dram_tensor("out", (C, ALL), mybir.dt.float32, kind="ExternalOutput").ap()
    bass_local_attention_then_deformable_conv(
        nc, d["x"], d["cf"], d["wom"],
        {k: d[k] for k in ("bcast", "sely", "selx", "selm")}, {"y": d["rowsy"], "x": d["rowsx"]}, out)
    r = run(nc, [{"in_" + k: v for k, v in arrays.items()}], core_ids=[0])
    y = r.results[0]["out"].reshape(C, J, HALVES, H, W)
    return np.ascontiguousarray(y.transpose(2, 1, 0, 3, 4)).reshape(B, C, H, W)
```

```python
import concourse.bass as bass
from concourse import mybir
from contextlib import ExitStack

B, C, H, W = 8, 64, 16, 16
HW = H * W
HALVES = 2
J = B // HALVES
P = HALVES * C
N = J * HW
ALL = B * HW
TAPS = 9
PH, PW = H + 2, W + 2
HEADS, HD = 8, 8
SCALE = float(HD) ** -0.5
EPS = 1e-5
GC = 2
DG = 4
CG = C // DG
PAIRS = (TAPS + 1) // 2
OM = 3 * DG * TAPS
ND = DG * TAPS
STACK = 3 * ND
STRIP = 4
STRIPS = H // STRIP
WROWS = P // W
REACH = 2
SHIFTS = 5
WINS = 3 * STRIPS
SROWS = (STRIPS - 1) * STRIP + 2 + WROWS
FIRST_ROW = -(1 + REACH) - WROWS * (SHIFTS // 2)
TROWS = WROWS * (SHIFTS - 1) + SROWS
UNITS = PAIRS * DG
AHEAD = 2
AHEAD_X = 3
UP = UNITS * B + AHEAD
UPX = UNITS * B + AHEAD_X
HP = PAIRS * (B + 1)
BANK = 512
OUTS = ALL // BANK
RING = 2 * DG
SELECT_Y = {6: 0, 9: 1, 12: 2, 15: 3, 19: 4}
EXACT_Y = {8: 0, 11: 1, 14: 2, 17: 3}
VALUES = {5: 0, 9: 1, 13: 2, 17: 3, 19: 4}
HF = HW // 2
CHUNKS = 3
TC = TAPS // CHUNKS
CONV = [0, 2, 1, 3]
TAPSTEPS = 6
CENTER = SHIFTS // 2
POOL_TAPS = 3


def bass_local_attention_then_deformable_conv(nc, x, cf, wom, sel16, rows16, out):
    fp32, bf16, fp16 = mybir.dt.float32, mybir.dt.bfloat16, mybir.dt.float16
    i32, u16 = mybir.dt.int32, mybir.dt.uint16
    ALU = mybir.AluOpType
    ACT = mybir.ActivationFunctionType
    AX = mybir.AxisListType
    KEPT = [("gnp", P), ("gnd", P), ("ident", P), ("wfin", PAIRS * C), ("fold", C), ("bias", 8), ("table", SHIFTS)]
    ATTENTION = [("wqkv", 4 * P), ("w1", P), ("w2", P), ("wp", P), ("headsum", 2 * 32)]
    SELS = [("sely", PAIRS * P), ("selx", TAPS * P), ("selm", PAIRS * P), ("selpart", PAIRS * P)]

    with ExitStack() as ctx:
        def sb(name, shape, dt=fp32):
            return ctx.enter_context(nc.sbuf_tensor(name, shape, dt))

        def sem(name):
            return ctx.enter_context(nc.semaphore(name))

        kept = sb("kept", [P, sum(n for _, n in KEPT)])
        cst, at = {}, 0
        for name, n in KEPT:
            cst[name] = kept[:, at:at + n]
            at += n
        gnp, gnd, ident, bias, table = (cst[k] for k in ("gnp", "gnd", "ident", "bias", "table"))
        sel = {name: sb(f"s_{name}", [STACK + 2, n], bf16) for name, n in SELS}
        bcast = sb("bcast", [P, (DG + 2 * DG + 2 * J) * P], fp16)
        b2half = sb("b2half", [P, 1])
        minushalf = sb("minushalf", [P, J])
        halfstat = sb("halfstat", [P, 6 * J])
        meanvar = sb("meanvar", [P, 2 * J])
        pair = sb("pair", [P, 4 * J])
        one = sb("one", [P, 1])
        minusone = sb("minusone", [P, 1])
        half = sb("half", [P, 1])
        gap2 = sb("gap2", [P, J])
        vareps = sb("vareps", [P, J])
        rstd = sb("rstd", [P, J])

        PAD, XSW = J * PH * PW, 3 * CG

        def shared(name, first, then):
            size = max(sum(n for _, n in first), sum(n for _, n in then))
            words, views = sb(name, [P, size]), {}
            for names in (first, then):
                at = 0
                for key, n in names:
                    views[key] = words[:, at:at + n]
                    at += n
            return views

        W_ATT = sum(n for _, n in ATTENTION)
        m = shared("attention_weights", [("all", W_ATT)], [("vals1", PAIRS * HW)])
        attw, at = m["all"], 0
        for name, n in ATTENTION:
            cst[name] = attw[:, at:at + n]
            at += n
        m1 = shared("conv1_vals0", [("dup1", PAD)], [("vals0", PAIRS * HW)])
        vals = [m1["vals0"], m["vals1"]]
        m = shared("conv0_hx", [("womt", TAPSTEPS * OM), ("dup0", PAD)], [("hx", 4 * BANK)])
        womt, hx, dup = m["womt"], m["hx"], [m["dup0"], m1["dup1"]]
        m = shared("x_parts_smp", [("xin", N), ("x2", N)], [("smp", RING * BANK)])
        xin, x2, smp = m["xin"], m["x2"], m["smp"]
        parts = smp[0:OM, 4 * BANK:4 * BANK + 2 * 3 * BANK // 2].bitcast(bf16).rearrange("p (k i n) -> p k i n", k=2, i=3)
        rest = smp[0:OM, 7 * BANK:8 * BANK]
        om = smp[0:OM, 0:2 * BANK]
        m = shared("img_staged", [("img", PAD)], [("staged", J * SROWS * W)])
        img, staged = m["img"], m["staged"]
        m = shared("prod_maskb", [("prod", TAPS * N)], [("maskb", PAIRS * ALL)])
        prod, maskb = m["prod"], m["maskb"]

        WX, XS = J * WINS * P, WINS * DG * XSW
        arena = sb("arena", [P, WX + J * TROWS * W + 2 * XS])
        at = 0
        views = {}
        for key in ("pooled", "q", "chans", "hidden", "gate", "att"):
            views[key] = arena[:, at:at + N]
            at += N
        pooled, q, chans, hidden, gate, att = (views[k] for k in ("pooled", "q", "chans", "hidden", "gate", "att"))
        xT = arena[:, 0:WX + WINS * P]
        at = WX
        for key, n in (("kpad", PAD), ("vpad", PAD), ("hsum", J * PH * W), ("dlog", TAPS * HF), ("lmax", HF),
                       ("den", HF)):
            views[key] = arena[:, at:at + n]
            at += n
        kpad, vpad, hsum, dlog, lmax, den = (views[k] for k in ("kpad", "vpad", "hsum", "dlog", "lmax", "den"))
        tall = arena[:, WX:WX + J * TROWS * W]
        at = WX + J * TROWS * W
        xs = [arena[:, at + i * XS:at + (i + 1) * XS] for i in range(2)]

        stack = {k: sb(f"stack_{k}", [STACK + 2, ALL], bf16) for k in "ymx"}
        amax = sb("amax", [OM, len(CONV) + 1])
        far = sb("far", [1, 2])
        choice = sb("choice", [1, 1], i32)
        ybias = sb("ybias", [P, 1])
        distx = [sb(f"distx{i}", [P, BANK]) for i in range(2)]
        disty = [sb(f"disty{i}", [P, HW]) for i in range(2)]
        hatx = sb("hatx", [P, TAPS * HW], fp16)
        phi, plo = hatx[:, 0:TAPS * HF], hatx[:, TAPS * HF:2 * TAPS * HF]
        haty = sb("haty", [P, PAIRS * HW], fp16)
        acc = sb("acc", [P, (B + 1) * HW])
        x2seq = sb("x2seq", [C, ALL])

        ps = ctx.enter_context(nc.psum_tensor("ps", [P, 8 * BANK], fp32))

        def bank(i, n=1):
            return ps[:, i * BANK:(i + n) * BANK]

        def images(t, w=HW):
            return t[:, :].rearrange("p (j n) -> p j n", j=J)

        def padded(t):
            return t[:, :].rearrange("p (j r c) -> p j r c", j=J, r=PH)

        def shifted(t, tap):
            return padded(t)[:, :, tap // 3:tap // 3 + H, tap % 3:tap % 3 + W]

        def halfimages(ap, c):
            return grid(ap)[:, 2 * c:2 * c + 2]

        def grid(ap):
            return ap.rearrange("p (j r c) -> p j r c", j=J, r=H)

        s_x = [sem("s_x0"), sem("s_x1")]
        s_cst, s_wom, s_sel, s_rows = sem("s_cst"), sem("s_wom"), sem("s_sel"), sem("s_rows")
        s_zero = sem("s_zero")
        s_bn = sem("s_bn")
        s_kept, s_bcast = sem("s_kept"), sem("s_bcast")
        s_stats, s_pair, s_eps, s_rstd = sem("s_stats"), sem("s_pair"), sem("s_eps"), sem("s_rstd")
        s_pool, s_qkv, s_ev, s_chans = sem("s_pool"), sem("s_qkv"), sem("s_ev"), sem("s_chans")
        s_up, s_hid, s_down, s_gate = sem("s_up"), sem("s_hid"), sem("s_down"), sem("s_gate")
        s_prod, s_prodpool, s_log, s_dlog, s_exp, s_prob, s_hi, s_lo = (sem(n) for n in (
            "s_prod", "s_prodpool", "s_log", "s_dlog", "s_exp", "s_prob", "s_hi", "s_lo"))
        s_pb, s_pv, s_pbcopy, s_pvpool, s_pvsum, s_att, s_attn, s_proj = (sem(n) for n in (
            "s_pb", "s_pv", "s_pbcopy", "s_pvpool", "s_pvsum", "s_att", "s_attn", "s_proj"))
        s_dve = sem("s_dve")
        s_x2, s_x2seq = sem("s_x2"), sem("s_x2seq")
        s_tall, s_dup0, s_dup1 = sem("s_tall"), sem("s_dup0"), sem("s_dup1")
        s_conv, s_omraw, s_om, s_parts = (sem(n) for n in ("s_conv", "s_omraw", "s_om", "s_parts"))
        s_mstack = [sem(f"s_mstack{n}") for n in range(len(CONV))]
        s_stack = [sem(f"s_stack{n}") for n in range(len(CONV))]
        s_amaxed = sem("s_amaxed")
        s_amax, s_amaxT, s_choice = sem("s_amax"), sem("s_amaxT"), sem("s_choice")
        s_mb, s_maska, s_maskd = sem("s_mb"), sem("s_maska"), sem("s_maskd")
        s_staged, s_tr, s_xTa, s_xTd, s_xs, s_ybias = (sem(n) for n in (
            "s_staged", "s_tr", "s_xTa", "s_xTd", "s_xs", "s_ybias"))
        s_selx, s_sely, s_absx, s_absy, s_ux, s_uy = (sem(n) for n in (
            "s_selx", "s_sely", "s_absx", "s_absy", "s_ux", "s_uy"))
        s_cx, s_cy, s_hatx, s_haty = sem("s_cx"), sem("s_cy"), sem("s_hatx"), sem("s_haty")
        s_bx, s_by, s_hx, s_smp, s_smpfree = (sem(n) for n in ("s_bx", "s_by", "s_hx", "s_smp", "s_smpfree"))
        s_vals, s_fin, s_acc, s_fold, s_y, s_out = (sem(n) for n in (
            "s_vals", "s_fin", "s_acc", "s_fold", "s_y", "s_out"))

        ONE = 1
        FROM_ONE = [s_tr, s_hatx, s_haty, s_smp, s_absx, s_absy, s_hx, s_acc]

        QKV = [(0, 0), (1, 0), (0, 1), (1, 1), (3, 0), (3, 1), (2, 0), (2, 1)]
        QK = 4
        BORDER = [2, 0, 3, 1] + list(range(4, TAPS))
        PB = [4, 6, 0]

        block = ctx.enter_context(nc.Block())

        HATS = {2: (0, 2, 4), 3: (1, 3)}
        SLICES = len(CONV) * PAIRS
        DIRECT = SLICES - 2 * PAIRS
        LAST = SLICES - PAIRS
        BY_VECTOR = [1, 3, 6, 8, 10, 12, 16, 18]

        def slice_bank(n):
            return bank(n % 4 if n < LAST else (4, 5, 7)[(n - LAST) % 3])

        def taken(eng, n):
            by_vector = sum(m <= n for m in BY_VECTOR)
            eng.wait_ge(s_maska, n + 1 - by_vector)
            if by_vector:
                eng.wait_ge(s_maskd, by_vector)

        def for_engine(name, first, end):
            return [n for n in range(first, end) if (n in BY_VECTOR) == (name == "vector")]

        def mask_slice(n):
            c = CONV[n // PAIRS]
            return maskb[:, n % PAIRS * ALL + c * BANK:][:, 0:BANK]

        @block.sync
        def _(sp):
            for c in range(2):
                sp.dma_start(xin[:, c * BANK:(c + 1) * BANK], x[:, c * BANK:(c + 1) * BANK]).then_inc(s_x[c], 16)
            sp.dma_start(bcast[:, :], sel16["bcast"]).then_inc(s_bcast, 16)
            sp.dma_start(womt[:, :], wom).then_inc(s_wom, 16)
            for name, n in SELS:
                sp.dma_start(sel[name][:, :].bitcast(u16), sel16[name]).then_inc(s_sel, 16)
            for k in "ymx":
                sp.dma_start(stack[k][STACK:STACK + 2, :].bitcast(u16), rows16["x" if k == "x" else "y"]).then_inc(s_rows, 16)
            sp.wait_ge(s_x2, 2)
            for h in range(HALVES):
                sp.dma_start(x2seq[:, :].rearrange("c (j h n) -> c j h n", j=J, h=HALVES)[:, :, h, :],
                             images(x2)[h * C:(h + 1) * C]).then_inc(s_x2seq, 16)
            for n, c in enumerate(CONV):
                sp.wait_ge(s_parts, n + 1)
                for row, k in enumerate("myx"):
                    if k == "m" and n * PAIRS >= DIRECT:
                        continue
                    for i in range(3):
                        sp.dma_start(stack[k][i * ND:(i + 1) * ND, c * BANK:(c + 1) * BANK],
                                     parts[row * ND:(row + 1) * ND, n % 2, i]).then_inc(
                                         s_mstack[n] if k == "m" else s_stack[n], 16)
            for n, c in enumerate([OUTS - 1] + list(range(OUTS - 1))):
                sp.wait_ge(s_y, n + 1)
                sp.dma_start(out[:, c * BANK:(c + 1) * BANK], x2seq[:, c * BANK:(c + 1) * BANK]).then_inc(s_out, 16)
            sp.wait_ge(s_out, 16 * OUTS)

        @block.gpsimd
        def _(pool):
            nc.gpsimd.memset(img[:, :], 0.0).then_inc(s_zero, 1)
            nc.gpsimd.memset(hsum[:, :], 0.0).then_inc(s_zero, 1)
            nc.gpsimd.memset(minushalf[:, :], -0.5).then_inc(s_zero, 1)
            nc.gpsimd.memset(kpad[:, :], 0.0).then_inc(s_zero, 1)
            nc.gpsimd.memset(vpad[:, :], 0.0).then_inc(s_zero, 1)
            pool.wait_ge(s_zero, 5)
            pool.wait_ge(s_eps, 1)
            nc.gpsimd.tensor_tensor(rstd[:, :], vareps[:, :], minushalf[:, :], ALU.pow).then_inc(s_rstd, 1)
            nc.gpsimd.memset(one[:, :], 1.0).then_inc(s_zero, 1)
            nc.gpsimd.memset(acc[:, :], 0.0).then_inc(s_zero, 1)
            for i in range(2):
                nc.gpsimd.memset(dup[i], 0.0).then_inc(s_zero, 1)
            nc.gpsimd.memset(minusone[:, :], -1.0).then_inc(s_zero, 1)
            nc.gpsimd.memset(half[:, :], 0.5).then_inc(s_zero, 1)
            for counter in FROM_ONE:
                pool.sem_inc(counter, ONE)
            pool.sem_inc(s_smpfree, RING)
            for c in range(2):
                pool.wait_ge(s_ev, 2 + 2 * c)
                for t in range(TAPS - POOL_TAPS, TAPS):
                    nc.gpsimd.tensor_tensor(halfimages(prod[:, t * N:(t + 1) * N], c), halfimages(q[:, :], c),
                                            shifted(kpad, t)[:, 2 * c:2 * c + 2], ALU.mult).then_inc(s_prodpool, 1)
            pool.wait_ge(s_ev, 8)
            for t in range(2):
                pool.wait_ge(s_pbcopy, t + 1)
                nc.gpsimd.tensor_tensor(grid(prod[:, t * N:(t + 1) * N]), grid(prod[:, t * N:(t + 1) * N]),
                                        shifted(vpad, t), ALU.mult).then_inc(s_pvpool, 1)
            pool.wait_ge(s_pvpool, 2)
            nc.gpsimd.tensor_tensor(prod[:, 0:N], prod[:, 0:N], prod[:, N:2 * N], ALU.add).then_inc(s_pvpool, 1)
            pool.wait_ge(s_pv, 6)
            nc.gpsimd.tensor_tensor(prod[:, 6 * N:7 * N], prod[:, 6 * N:7 * N], prod[:, 7 * N:8 * N],
                                    ALU.add).then_inc(s_pvpool, 1)
            pool.wait_ge(s_x2, 2)
            nc.gpsimd.memset(tall[:, :], 0.0).then_inc(s_zero, 1)
            pool.wait_ge(s_eps, 2)
            nc.gpsimd.tensor_tensor(rstd[:, :], vareps[:, :], minushalf[:, :], ALU.pow).then_inc(s_rstd, 1)
            for i in range(2):
                nc.gpsimd.memset(xs[i][:, :], 0.0).then_inc(s_zero, 1)
            pool.wait_ge(s_zero, 14)
            nc.gpsimd.memset(vals[1][:, :], 0.0).then_inc(s_vals, 1)

            def spread(i, src_j, h, first=False):
                src = xT[:, bass.ds(src_j * (WINS * P), WINS * P)].rearrange(
                    "p (w h g c) -> p w h g c", w=WINS, h=HALVES, g=DG)[:, :, h, :, :]
                dst = xs[i][:, :].rearrange("p (w g c) -> p w g c", w=WINS, g=DG)[:, :, :, CG:2 * CG]
                if first:
                    ones = one[:, :].unsqueeze(2).unsqueeze(3).to_broadcast([P, WINS, DG, CG])
                    return nc.gpsimd.tensor_tensor(dst, src, ones, ALU.mult)
                return nc.gpsimd.tensor_copy(dst, src)

            def low_parts(p, i, n):
                t = 2 * p
                w = HW * min(2, TAPS - t)
                pool.wait_ge(s_ux, n)
                pool.wait_ge(s_haty, ONE + n - 1)
                nc.gpsimd.tensor_tensor(hatx[C:P, t * HW:t * HW + w], distx[i][C:P, 0:w],
                                        hatx[C:P, t * HW:t * HW + w], ALU.add).then_inc(s_hatx, 1)
                pool.wait_ge(s_uy, n)
                pool.wait_ge(s_hatx, ONE + n)
                nc.gpsimd.tensor_tensor(haty[:, p * HW:(p + 1) * HW], disty[i][:, :],
                                        minusone[:, :].to_broadcast([P, HW]), ALU.mult).then_inc(s_cy, 1)
                pool.wait_ge(s_cy, n)
                nc.gpsimd.tensor_tensor(haty[C:P, p * HW:(p + 1) * HW], disty[i][C:P, :],
                                        haty[C:P, p * HW:(p + 1) * HW], ALU.add).then_inc(s_haty, 1)

            def prologue(it):
                pool.wait_ge(s_xTa, (it + 1) * 6)
                pool.wait_ge(s_xTd, (it + 1) * 6)
                spread(0, 0, 0, first=True).then_inc(s_xs, 1)
                pool.wait_ge(s_xs, it * (B + 1) + 1)
                for p in range(PAIRS - 1):
                    low_parts(p, p % 2, it * HP + p + 1)

            prologue(0)
            pool.wait_ge(s_choice, 1)
            passes = pool.value_load(choice[0:1, 0:1], min_val=1, max_val=SHIFTS)
            with pool.Fori(0, passes) as it:
                with pool.If(it > 0):
                    pool.wait_ge(s_haty, ONE + it * HP)
                    shift = nc.s_assert_within((it - 1) + it // (CENTER + 1), 0, SHIFTS - 1)
                    nc.gpsimd.tensor_copy(images(staged), images(tall)[:, :, bass.ds(shift * (WROWS * W), SROWS * W)]
                                          ).then_inc(s_staged, 1)
                    pool.wait_ge(s_smpfree, RING + it * (UNITS * B))
                    prologue(it)
                with pool.Fori(0, J) as j:
                    for h in range(HALVES):
                        low_parts(PAIRS - 1, h, it * HP + j * (2 * PAIRS) + (h + 1) * PAIRS)
                        pool.wait_ge(s_smpfree, RING + it * (UNITS * B) + j * (2 * UNITS) + h * UNITS)
                        pool.wait_ge(s_haty, ONE + it * HP + j * (2 * PAIRS) + (h + 1) * PAIRS)
                        spread(1 - h, j + h, 1 - h).then_inc(s_xs, 1)
                        pool.wait_ge(s_xs, it * (B + 1) + j * 2 + (h + 2))
                        for p in range(PAIRS - 1):
                            low_parts(p, (h + 1 + p) % 2, it * HP + j * (2 * PAIRS) + ((h + 1) * PAIRS + p + 1))
                low_parts(PAIRS - 1, 0, (it + 1) * HP)

        @block.scalar
        def _(act):
            act.dma_start(kept[:, :], cf[:, 0:kept.shape[1]]).then_inc(s_kept, 16)
            act.dma_start(attw, cf[:, kept.shape[1]:]).then_inc(s_cst, 16)
            act.wait_ge(s_kept, 16)
            act.wait_ge(s_zero, 5)
            def out_of_qkv(n):
                t, c = QKV[n]
                dst = {0: halfimages(q[:, :], c), 1: shifted(kpad, 4)[:, 2 * c:2 * c + 2],
                       2: shifted(vpad, 4)[:, 2 * c:2 * c + 2], 3: halfimages(chans[:, :], c)}[t]
                act.wait_ge(s_qkv, n + 1)
                nc.scalar.activation(dst, bank(2 * t + c).rearrange("p (j r c) -> p j r c", j=2, r=H), ACT.Identity,
                                     bias=bias[:, t:t + 1], scale=1.0 / TAPS).then_inc(s_ev, 1)

            for n in range(QK + 2):
                out_of_qkv(n)
            for k in range(CHUNKS):
                act.wait_ge(s_dlog, k + 1)
                e = dlog[:, k * TC * HF:(k + 1) * TC * HF]
                nc.scalar.activation(e, e, ACT.Exp, scale=SCALE).then_inc(s_exp, 1)
            for n in range(QK + 2, len(QKV)):
                out_of_qkv(n)
            for c in range(2):
                act.wait_ge(s_up, c + 1)
                nc.scalar.activation(hidden[:, c * BANK:(c + 1) * BANK], bank(6 + c), ACT.Relu,
                                     bias=bias[:, 4:5]).then_inc(s_hid, 1)
            act.wait_ge(s_chans, 1)
            for c in range(2):
                act.wait_ge(s_down, c + 1)
                nc.scalar.activation(gate[:, c * BANK:(c + 1) * BANK], bank(6 + c), ACT.Tanh, bias=b2half[:, :],
                                     scale=0.5).then_inc(s_gate, 1)
            for k in range(CHUNKS):
                act.wait_ge(s_prob, k + 1)
                cols = slice(k * TC * HF, (k + 1) * TC * HF)
                nc.scalar.copy(phi[:, cols], dlog[:, cols]).then_inc(s_hi, 1)
            for n in range(2):
                pos = BORDER.index(n)
                act.wait_ge(s_pb, pos + 1)
                nc.scalar.copy(prod[:, n * N:(n + 1) * N], bank(PB[pos % 3], 2)).then_inc(s_pbcopy, 1)
            act.wait_ge(s_tall, J)
            act.wait_ge(s_zero, 9)
            source = images(tall)[C:P, :, -FIRST_ROW * W:(-FIRST_ROW + H) * W].rearrange("p j (r c) -> p j r c", r=H)
            nc.scalar.copy(shifted(dup[1], 4)[0:C], source).then_inc(s_dup1, 1)
            nc.scalar.copy(shifted(dup[1], 3)[C:P], source).then_inc(s_dup1, 1)

            def offsets(n):
                act.wait_ge(s_conv, n + 1)
                if n >= 2:
                    act.wait_ge(s_amaxed, n - 1)
                o = om[:, n % 2 * BANK:(n % 2 + 1) * BANK]
                nc.scalar.activation(o, bank(4 + n % 2 * 2)[0:OM], ACT.Identity, bias=bias[0:OM, 7:8]).then_inc(s_omraw, 1)
                act.wait_ge(s_omraw, n + 1)
                nc.scalar.activation(o[0:ND], o[0:ND], ACT.Tanh, scale=0.5).then_inc(s_om, 1)

            def mask_out(n):
                act.wait_ge(s_mb, n + 1)
                if n < DIRECT:
                    ins = nc.scalar.copy(mask_slice(n), slice_bank(n))
                else:
                    ins = nc.scalar.activation(mask_slice(n), slice_bank(n), ACT.Identity, bias=half[:, :])
                ins.then_inc(s_maska, 1)

            def evac(slot, n, bank_, w, waits_smp):
                act.wait_ge(s_bx, n)
                act.wait_ge(s_smp, ONE + waits_smp)
                nc.scalar.copy(hx[:, slot * BANK:slot * BANK + w], bank(bank_)[:, 0:w]).then_inc(s_hx, 1)

            def distance_x(p, i, n, free):
                w = HW * min(2, TAPS - 2 * p)
                act.wait_ge(s_selx, n)
                act.wait_ge(s_hatx, ONE + free)
                nc.scalar.activation(distx[i][:, 0:w], bank(5)[:, 0:w], ACT.Abs).then_inc(s_absx, 1)

            def distance_y(p, i, n, free):
                act.wait_ge(s_sely, n)
                act.wait_ge(s_haty, ONE + free)
                nc.scalar.activation(disty[i][:, :], bank(7)[:, 0:HW], ACT.Abs, bias=ybias[:, :]).then_inc(s_absy, 1)

            def hat_x(p, i, n):
                t = 2 * p
                w = HW * min(2, TAPS - t)
                act.wait_ge(s_absx, ONE + n)
                nc.scalar.activation(hatx[:, t * HW:t * HW + w], distx[i][:, 0:w], ACT.Relu, bias=1.0,
                                     scale=-1.0).then_inc(s_cx, 1)

            def windows_out(it):
                for g in range(0, 12, 2):
                    act.wait_ge(s_tr, ONE + it * 12 + (g + 1))
                    nc.scalar.copy(xT[:, g * BANK:(g + 1) * BANK], bank(g % 4)).then_inc(s_xTa, 1)

            def hats(p, it):
                n = it * HP + p + 1
                free = it * HP + max(p - 1, 0)
                distance_x(p, p % 2, n, free)
                distance_y(p, p % 2, n, free)
                hat_x(p, p % 2, n)

            offsets(0)
            windows_out(0)
            offsets(1)
            act.wait_ge(s_ybias, 1)
            hat = 0
            for step in (2, 3):
                for p in range(PAIRS):
                    if p == PAIRS - 1:
                        offsets(step)
                    if p in HATS[step]:
                        hats(hat, 0)
                        hat += 1
                    for n in for_engine("scalar", (step - 2) * PAIRS + p, (step - 2) * PAIRS + p + 1):
                        mask_out(n)
            for n in for_engine("scalar", 2 * PAIRS, LAST):
                mask_out(n)
            for g in range(AHEAD_X):
                evac(g, g + 1, g % 2, BANK, 0)
            for n in for_engine("scalar", LAST, SLICES):
                mask_out(n)
            act.wait_ge(s_choice, 1)
            passes = act.value_load(choice[0:1, 0:1], min_val=1, max_val=SHIFTS)
            with act.Fori(0, passes) as it:
                with act.If(it > 0):
                    windows_out(it)
                    act.wait_ge(s_ybias, it + 1)
                    for p in range(PAIRS):
                        hats(p, it)
                        if p == 0:
                            for g in range(AHEAD_X):
                                evac(g, it * UPX + g + 1, g % 2, BANK, it * UP)
                with act.Fori(0, J) as j:
                    for h in range(HALVES):
                        for u in range(UNITS):
                            g = h * UNITS + u + AHEAD_X
                            p = (u + AHEAD_X) % UNITS // DG
                            evac(g % 4, it * UPX + j * (2 * UNITS) + g + 1, g % 2, HW * min(2, TAPS - 2 * p),
                                 it * UP + j * (2 * UNITS) + g - 3)
                            n = it * HP + j * (2 * PAIRS) + ((h + 1) * PAIRS + u // 4 + 1)
                            i = (h + 1 + u // 4) % 2
                            if u % 4 == 2:
                                distance_x(u // 4, i, n, n - 2)
                            if u in SELECT_Y:
                                p = SELECT_Y[u]
                                ny = it * HP + j * (2 * PAIRS) + ((h + 1) * PAIRS + p + 1)
                                distance_y(p, (h + 1 + p) % 2, ny, ny - 2)
                            if u % 4 == 3:
                                hat_x(u // 4, i, n)

        @block.vector
        def _(dve):
            chain = [0]

            def link(ins):
                chain[0] += 1
                ins.then_inc(s_dve, 1)
                dve.wait_ge(s_dve, chain[0])

            def norm_stats(src, j):
                for i in (j, j + 1):
                    nc.vector.bn_stats(halfstat[:, 6 * i:6 * i + 6], src[:, i * HW:(i + 1) * HW]).then_inc(s_bn, 1)
                n = bn[0] = bn[0] + 2
                dve.wait_ge(s_bn, n)
                for i in (j, j + 1):
                    nc.vector.bn_aggr(meanvar[:, 2 * i:2 * i + 2], halfstat[:, 6 * i:6 * i + 6]).then_inc(s_stats, 1)

            def norm(src, n):
                dve.wait_ge(s_pair, n)
                link(nc.vector.tensor_copy(pair[:, :], bank(7)[:, 0:4 * J]))
                gap = pair[:, 2 * J:4 * J].rearrange("p (j s) -> p j s", s=2)[:, :, 0]
                var = pair[:, 0:2 * J].rearrange("p (j s) -> p j s", s=2)[:, :, 1]
                link(nc.vector.tensor_tensor(gap2[:, :], gap, gap, ALU.mult))
                nc.vector.scalar_tensor_tensor(vareps[:, :], gap2[:, :], EPS, var, ALU.add, ALU.add).then_inc(s_eps, 1)
                dve.wait_ge(s_rstd, n)

            def normalise(dst, src, j, rows=slice(0, P)):
                return nc.vector.tensor_scalar(dst, grid(src[:, :])[rows, j], pair[rows, 2 * j:2 * j + 1],
                                               rstd[rows, j:j + 1], ALU.subtract, ALU.mult)

            bn = [0]
            for c in range(2):
                dve.wait_ge(s_x[c], 16)
                norm_stats(xin, 2 * c)
            dve.wait_ge(s_zero, 2)
            norm(xin, 1)
            for j in range(J):
                ins = normalise(shifted(img, 4)[:, j], xin, j)
            link(ins)
            for c in range(2):
                im = padded(img)[:, 2 * c:2 * c + 2]
                hs = hsum[:, :].rearrange("p (j r c) -> p j r c", j=J, r=PH)[:, 2 * c:2 * c + 2]
                mid = hs[:, :, 1:H + 1, :]
                po = halfimages(pooled[:, :], c)
                link(nc.vector.tensor_tensor(mid, im[:, :, 1:H + 1, 0:W], im[:, :, 1:H + 1, 1:W + 1], ALU.add))
                link(nc.vector.tensor_tensor(mid, mid, im[:, :, 1:H + 1, 2:W + 2], ALU.add))
                link(nc.vector.tensor_tensor(po, hs[:, :, 0:H, :], hs[:, :, 1:H + 1, :], ALU.add))
                nc.vector.tensor_tensor(po, po, hs[:, :, 2:H + 2, :], ALU.add).then_inc(s_pool, 1)
            dve.wait_ge(s_kept, 16)
            nc.vector.tensor_scalar(b2half[:, :], bias[:, 5:6], 0.5, None, ALU.mult).then_inc(s_chans, 1)
            for c in range(2):
                dve.wait_ge(s_ev, 2 + 2 * c)
                for t in range(TAPS - POOL_TAPS):
                    nc.vector.tensor_tensor(halfimages(prod[:, t * N:(t + 1) * N], c), halfimages(q[:, :], c),
                                            shifted(kpad, t)[:, 2 * c:2 * c + 2], ALU.mult).then_inc(s_prod, 1)
            dve.wait_ge(s_log, 2 * TAPS)
            logits = ps[:, 0:TAPS * HF].rearrange("p (t n) -> p t n", t=TAPS)
            d3 = dlog[:, :].rearrange("p (t n) -> p t n", t=TAPS)
            link(nc.vector.tensor_reduce(lmax[:, :], logits.rearrange("p t n -> p n t"), AX.X, ALU.max))
            for k in range(CHUNKS):
                taps = slice(k * TC, (k + 1) * TC)
                nc.vector.tensor_tensor(d3[:, taps], logits[:, taps], lmax[:, :].unsqueeze(1).to_broadcast([P, TC, HF]),
                                        ALU.subtract).then_inc(s_dlog, 1)
            dve.wait_ge(s_exp, CHUNKS)
            link(nc.vector.tensor_reduce(den[:, :], d3.rearrange("p t n -> p n t"), AX.X, ALU.add))
            link(nc.vector.reciprocal(den[:, :], den[:, :]))
            for k in range(CHUNKS):
                taps = slice(k * TC, (k + 1) * TC)
                nc.vector.tensor_tensor(d3[:, taps], d3[:, taps], den[:, :].unsqueeze(1).to_broadcast([P, TC, HF]),
                                        ALU.mult).then_inc(s_prob, 1)
            for k in range(CHUNKS):
                dve.wait_ge(s_hi, k + 1)
                cols = slice(k * TC * HF, (k + 1) * TC * HF)
                dve.wait_ge(s_prob, k + 1)
                nc.vector.tensor_tensor(plo[:, cols], dlog[:, cols], phi[:, cols], ALU.subtract).then_inc(s_lo, 1)
            dve.wait_ge(s_ev, 8)

            def pv_sum(a, b, n):
                dve.wait_ge(s_pv, n)
                nc.vector.tensor_tensor(prod[:, a * N:(a + 1) * N], prod[:, a * N:(a + 1) * N],
                                        prod[:, b * N:(b + 1) * N], ALU.add).then_inc(s_pvsum, 1)

            for t in range(2, TAPS):
                pos = BORDER.index(t)
                dve.wait_ge(s_pb, pos + 1)
                nc.vector.tensor_tensor(grid(prod[:, t * N:(t + 1) * N]), grid(bank(PB[pos % 3], 2)),
                                        shifted(vpad, t), ALU.mult).then_inc(s_pv, 1)
                if t in (3, 5):
                    pv_sum(t - 1, t, t - 1)
            dve.wait_ge(s_gate, 2)
            link(nc.vector.tensor_scalar(gate[:, :], gate[:, :], 0.5, 1.5, ALU.mult, ALU.add))
            for c in range(2):
                dve.wait_ge(s_att, c + 1)
                cols = slice(c * BANK, (c + 1) * BANK)
                nc.vector.tensor_tensor(att[:, cols], bank(2 + c), gate[:, cols], ALU.mult).then_inc(s_attn, 1)
            for c in range(2):
                cols = slice(c * BANK, (c + 1) * BANK)
                dve.wait_ge(s_proj, c + 1)
                nc.vector.scalar_tensor_tensor(x2[:, cols], bank(c), bias[:, 6:7], xin[:, cols], ALU.add,
                                               ALU.add).then_inc(s_x2, 1)
            for c in range(2):
                dve.wait_ge(s_x2, c + 1)
                norm_stats(x2, 2 * c)
            norm(x2, 2)
            dve.wait_ge(s_zero, 12)
            low = slice(0, C)
            for part in range(2):
                for j in (2 * part, 2 * part + 1):
                    normalise(shifted(dup[0], 4)[low, j], x2, j, low)
                    ins = normalise(shifted(dup[0], 3)[C:P, j], x2, j, low)
                ins.then_inc(s_dup0, 1)
                if part == 0:
                    for j in range(J):
                        normalise(tall[:, :].rearrange("p (j r c) -> p j r c", j=J, r=TROWS)[
                            :, j, -FIRST_ROW:-FIRST_ROW + H, :], x2, j).then_inc(s_tall, 1)
            dve.wait_ge(s_x2seq, 16 * HALVES)
            dve.wait_ge(s_dup0, 2)

            def offset_parts(n):
                dve.wait_ge(s_om, n + 1)
                if n >= 2:
                    dve.wait_ge(s_mstack[n - 2], 16 * 3)
                    dve.wait_ge(s_stack[n - 2], 16 * 6)
                o = om[:, n % 2 * BANK:(n % 2 + 1) * BANK]
                part = [parts[:, n % 2, i] for i in range(3)]
                link(nc.vector.tensor_copy(part[0], o))
                link(nc.vector.tensor_tensor(rest, o, part[0], ALU.subtract))
                link(nc.vector.tensor_copy(part[1], rest))
                nc.vector.tensor_tensor(part[2], rest, part[1], ALU.subtract).then_inc(s_parts, 1)
                nc.vector.tensor_reduce(amax[:, n:n + 1], o, AX.X, ALU.max,
                                        apply_absolute_value=True).then_inc(s_amaxed, 1)

            def mask_out(n):
                dve.wait_ge(s_mb, n + 1)
                if n < DIRECT:
                    ins = nc.vector.tensor_copy(mask_slice(n), slice_bank(n))
                else:
                    ins = nc.vector.tensor_scalar(mask_slice(n), slice_bank(n), 0.5, None, ALU.add)
                ins.then_inc(s_maskd, 1)

            def exact_x(p, i, n):
                w = HW * min(2, TAPS - 2 * p)
                dve.wait_ge(s_cx, n)
                nc.vector.tensor_scalar(distx[i][:, 0:w], distx[i][:, 0:w], 1.0, 1.0, ALU.min,
                                        ALU.subtract).then_inc(s_ux, 1)

            def exact_y(p, i, n):
                dve.wait_ge(s_absy, ONE + n)
                nc.vector.tensor_scalar(disty[i][:, :], disty[i][:, :], 1.0, 1.0, ALU.min,
                                        ALU.subtract).then_inc(s_uy, 1)

            def sample(g, w, n, nx, place):
                s, r = g % 4, g % RING
                dve.wait_ge(s_by, n)
                dve.wait_ge(s_hx, ONE + nx)
                dve.wait_ge(s_smpfree, place)
                nc.vector.tensor_tensor(smp[:, r * BANK:r * BANK + w], bank(2 + g % 2)[:, 0:w],
                                        hx[:, s * BANK:s * BANK + w], ALU.mult).then_inc(s_smp, 1)

            def accumulate(slot, n):
                dve.wait_ge(s_fin, n)
                dve.wait_ge(s_acc, ONE + n - 1)
                a = acc[:, bass.ds(slot * HW, HW)]
                nc.vector.tensor_tensor(a, bank(7)[:, 0:HW], a, ALU.add).then_inc(s_acc, 1)

            def windows_out(it):
                for g in range(1, 12, 2):
                    dve.wait_ge(s_tr, ONE + it * 12 + (g + 1))
                    nc.vector.tensor_copy(xT[:, g * BANK:(g + 1) * BANK], bank(g % 4)).then_inc(s_xTd, 1)

            offset_parts(0)
            nc.vector.tensor_copy(ybias[:, :], table[:, 0:1]).then_inc(s_ybias, 1)
            windows_out(0)
            offset_parts(1)
            for step in (2, 3):
                for n in for_engine("vector", (step - 2) * PAIRS, (step - 1) * PAIRS):
                    mask_out(n)
                for p in range(len(HATS[2])) if step == 2 else range(len(HATS[2]), PAIRS - 1):
                    exact_x(p, p % 2, p + 1)
                    exact_y(p, p % 2, p + 1)
                if step == 3:
                    for n in for_engine("vector", 2 * PAIRS, LAST):
                        mask_out(n)
                offset_parts(step)
            dve.wait_ge(s_amaxed, len(CONV))
            nc.vector.tensor_reduce(amax[:, len(CONV):], amax[:, 0:len(CONV)], AX.X, ALU.max).then_inc(s_amax, 1)
            for g in range(AHEAD):
                sample(g, BANK, g + 1, g + 1, g + 1)
            dve.wait_ge(s_amaxT, 1)
            link(nc.vector.tensor_reduce(far[0:1, 0:1], bank(6)[0:1, 0:OM], AX.X, ALU.max))
            link(nc.vector.tensor_scalar(far[0:1, 1:2], far[0:1, 0:1], float(REACH), float(SHIFTS - 1), ALU.is_gt,
                                         ALU.mult))
            nc.vector.tensor_scalar(choice[0:1, 0:1], far[0:1, 1:2], 1.0, None, ALU.add).then_inc(s_choice, 1)
            for n in for_engine("vector", LAST, SLICES):
                mask_out(n)
            dve.wait_ge(s_choice, 1)
            passes = dve.value_load(choice[0:1, 0:1], min_val=1, max_val=SHIFTS)
            for n in range(len(CONV)):
                dve.wait_ge(s_stack[n], 16 * 6)
            taken(dve, SLICES - 1)
            with dve.Fori(0, passes) as it:
                with dve.If(it > 0):
                    dve.wait_ge(s_absy, ONE + it * HP)
                    nc.vector.tensor_copy(ybias[:, :], table[:, bass.ds(nc.s_assert_within(it, 0, SHIFTS - 1), 1)]
                                          ).then_inc(s_ybias, 1)
                    windows_out(it)
                    for p in range(PAIRS - 1):
                        exact_x(p, p % 2, it * HP + p + 1)
                        exact_y(p, p % 2, it * HP + p + 1)
                    for g in range(AHEAD):
                        sample(g, BANK, it * UP + g + 1, it * UPX + g + 1, it * (UNITS * B) + (g + 1))
                with dve.Fori(0, J) as j:
                    for h in range(HALVES):
                        for u in range(UNITS):
                            g = h * UNITS + u + AHEAD
                            p = (u + AHEAD) % UNITS // DG
                            sample(g, HW * min(2, TAPS - 2 * p), it * UP + j * (2 * UNITS) + g + 1,
                                   it * UPX + j * (2 * UNITS) + g + 1, it * (UNITS * B) + j * (2 * UNITS) + (g + 1))
                            if u == 5:
                                accumulate(j * 2 + h, it * (B + 1) + j * 2 + (h + 1))
                            if u % 4 == 0:
                                exact_x((u // 4 - 1) % PAIRS, (h + u // 4) % 2,
                                        it * HP + j * (2 * PAIRS) + ((h + 1) * PAIRS + u // 4))
                            if u == 1:
                                exact_y(PAIRS - 1, h, it * HP + j * (2 * PAIRS) + ((h + 1) * PAIRS))
                            if u in EXACT_Y:
                                p = EXACT_Y[u]
                                exact_y(p, (h + 1 + p) % 2, it * HP + j * (2 * PAIRS) + ((h + 1) * PAIRS + p + 1))
                            if u in VALUES:
                                p = VALUES[u]
                                dve.wait_ge(s_smpfree, RING + it * (UNITS * B) + j * (2 * UNITS) + (h * UNITS + DG * (p + 1)))
                                nc.vector.tensor_tensor(
                                    vals[h][:, p * HW:(p + 1) * HW], bank(4 + 2 * ((h + p) % 2))[:, 0:HW],
                                    maskb[:, bass.ds(j * HW + (p * ALL + h * N), HW)], ALU.mult).then_inc(s_vals, 1)
                exact_x(PAIRS - 1, 0, (it + 1) * HP)
                exact_y(PAIRS - 1, 0, (it + 1) * HP)
                accumulate(B, it * (B + 1) + (B + 1))
            dve.wait_ge(s_acc, ONE + passes * (B + 1))
            last = OUTS - 1
            a = acc[:, HW + last * BANK:][:, 0:BANK]
            link(nc.vector.tensor_tensor(a[0:C], a[0:C], a[C:P], ALU.add))
            for n, c in enumerate([last] + list(range(last))):
                if n:
                    dve.wait_ge(s_fold, n)
                src = a[0:C] if c == last else bank(c)[0:C]
                xc = x2seq[:, c * BANK:(c + 1) * BANK]
                nc.vector.scalar_tensor_tensor(xc, src, 0.0, xc, ALU.max, ALU.add).then_inc(s_y, 1)

        @block.tensor
        def _(pe):
            def pair_stats(n):
                pe.wait_ge(s_stats, n * J)
                nc.tensor.matmul(bank(7)[:, 0:2 * J], gnp, meanvar[:, :], start=True, stop=True)
                nc.tensor.matmul(bank(7)[:, 2 * J:4 * J], gnd, meanvar[:, :], start=True, stop=True).then_inc(s_pair, 1)

            def dense(dst, w, src, c, signal):
                nc.tensor.matmul(bank(dst + c), w, src[:, c * BANK:(c + 1) * BANK], start=True, stop=True).then_inc(signal, 1)

            def keep_warm(products):
                for _ in range(products):
                    nc.tensor.matmul(bank(3), ident, kept[:, 0:BANK], start=True, stop=True)

            pe.wait_ge(s_kept, 16)
            pair_stats(1)
            keep_warm(4)
            pe.wait_ge(s_cst, 16)

            def qkv(t, c):
                pe.wait_ge(s_pool, c + 1)
                dense(2 * t, cst["wqkv"][:, t * P:(t + 1) * P], pooled, c, s_qkv)

            for t, c in QKV[:QK]:
                qkv(t, c)
            pe.wait_ge(s_ev, QK)

            def logits(t, c, n):
                if t < TAPS - POOL_TAPS:
                    pe.wait_ge(s_prod, n)
                else:
                    pe.wait_ge(s_prodpool, n)
                for part in range(2):
                    for j in (2 * c, 2 * c + 1):
                        ins = nc.tensor.matmul(ps[32 * j:32 * j + 32, t * HF:(t + 1) * HF],
                                               cst["headsum"][:, 32 * part:32 * part + 32],
                                               prod[:, t * N + j * HW + part * HF:][:, 0:HF], start=(part == 0),
                                               stop=(part == 1), skip_group_check=True)
                ins.then_inc(s_log, 1)

            mine = TAPS - POOL_TAPS
            for c in range(2):
                for k in range(POOL_TAPS):
                    logits(2 * k, c, c * mine + 2 * k + 1)
                    logits(2 * k + 1, c, c * mine + 2 * k + 2)
                    logits(mine + k, c, c * POOL_TAPS + k + 1)
            for t, c in QKV[QK:]:
                qkv(t, c)
            for c in range(2):
                pe.wait_ge(s_ev, QK + 1 + c)
                dense(6, cst["w1"], chans, c, s_up)
            for c in range(2):
                pe.wait_ge(s_hid, c + 1)
                dense(6, cst["w2"], hidden, c, s_down)
            keep_warm(2)
            pe.wait_ge(s_ev, len(QKV))
            pe.wait_ge(s_gate, 2)
            pe.wait_ge(s_bcast, 16)

            def pv_total(t, signal, count):
                pe.wait_ge(signal, count)
                for c in range(2):
                    ins = nc.tensor.matmul(bank(2 + c), ident, prod[:, t * N + c * BANK:][:, 0:BANK],
                                           start=(t == 2), stop=(t == 6))
                    if t == 6:
                        ins.then_inc(s_att, 1)

            for pos, t in enumerate(BORDER):
                pe.wait_ge(s_lo, t // TC + 1)
                if pos >= 3:
                    before = BORDER[pos - 3]
                    if before < 2:
                        pe.wait_ge(s_pbcopy, before + 1)
                    else:
                        pe.wait_ge(s_pv, before - 1)
                for i in range(2 * J):
                    c = (3 * DG + i) * P
                    for prob in (phi, plo):
                        ins = nc.tensor.matmul(ps[:, PB[pos % 3] * BANK + i * HF:][:, 0:HF], bcast[:, c:c + P],
                                               prob[:, t * HF:(t + 1) * HF], start=(prob is phi), stop=(prob is plo))
                ins.then_inc(s_pb, 1)
                if pos == 6:
                    pv_total(2, s_pvsum, 1)
            for sums in ((4, s_pvsum, 2), (0, s_pvpool, 3), (8, s_pv, 7), (6, s_pvpool, 4)):
                pv_total(*sums)
            for c in range(2):
                pe.wait_ge(s_attn, c + 1)
                dense(0, cst["wp"], att, c, s_proj)
            keep_warm(2)
            pair_stats(2)
            keep_warm(4)
            def select_x(p, image, n):
                pe.wait_ge(s_absx, ONE + n - 1)
                for t in range(2 * p, min(2 * p + 2, TAPS)):
                    ins = nc.tensor.matmul(bank(5)[:, t % 2 * HW:(t % 2 + 1) * HW], sel["selx"][:, t * P:(t + 1) * P],
                                           stack["x"][:, bass.ds(image * HW, HW)], start=True, stop=True)
                ins.then_inc(s_selx, 1)

            def select_y(p, image, n, nacc):
                pe.wait_ge(s_absy, ONE + n - 1)
                pe.wait_ge(s_acc, ONE + nacc)
                nc.tensor.matmul(bank(7)[:, 0:HW], sel["sely"][:, p * P:(p + 1) * P],
                                 stack["y"][:, bass.ds(image * HW, HW)], start=True, stop=True).then_inc(s_sely, 1)

            def select(p, image, n, nacc):
                select_x(p, image, n)
                select_y(p, image, n, nacc)

            def issue_x(g, unit, nhat, n):
                p, d = unit // DG, unit % DG
                taps = min(2, TAPS - 2 * p)
                if d == 0:
                    pe.wait_ge(s_hatx, ONE + nhat)
                pe.wait_ge(s_hx, ONE + n)
                nc.tensor.matmul(bank(g % 2)[:, 0:taps * HW], bcast[:, d * P:(d + 1) * P],
                                 hatx[:, 2 * p * HW:(2 * p + taps) * HW], start=True, stop=True).then_inc(s_bx, 1)

            def issue_y(g, unit, nhat, n):
                p, d = unit // DG, unit % DG
                taps = min(2, TAPS - 2 * p)
                if d == 0:
                    pe.wait_ge(s_haty, ONE + nhat)
                pe.wait_ge(s_smp, ONE + n)
                for a in range(taps):
                    at = (DG + 2 * d + a) * P
                    ins = nc.tensor.matmul(bank(2 + g % 2)[:, a * HW:(a + 1) * HW], bcast[:, at:at + P],
                                           haty[:, p * HW:(p + 1) * HW], start=True, stop=True)
                ins.then_inc(s_by, 1)

            def products(h, u, strips, n, nv):
                p, d0 = u // DG, u % DG
                taps = min(2, TAPS - 2 * p)
                if d0 == 0 and strips[0] == 0:
                    pe.wait_ge(s_vals, nv)
                if strips[0] == 0:
                    pe.wait_ge(s_smp, ONE + n)
                slot = bank(4 + 2 * ((h + p) % 2))
                for s in strips:
                    o = s * STRIP * W
                    for a in range(taps):
                        for d in (d0, d0 + 1):
                            w = ((s * 3 + (2 * p + a) // 3) * DG + d) * XSW + (CG if a == 0 else 0)
                            m = (h * UNITS + p * DG + d) % RING * BANK + a * HW + o
                            ins = nc.tensor.matmul(slot[32 * d:32 * d + 32, o:o + STRIP * W], xs[h][:, w:w + 2 * CG],
                                                   smp[:, m:m + STRIP * W], start=(a == 0 and s == 0),
                                                   stop=(a == taps - 1), skip_group_check=True)
                if strips[-1] == STRIPS - 1:
                    ins.then_inc(s_smpfree, 2)

            def final(i, pairs, n, nv, ny):
                if pairs[0] == 0:
                    pe.wait_ge(s_vals, nv)
                    pe.wait_ge(s_absy, ONE + ny)
                    pe.wait_ge(s_acc, ONE + n - 1)
                for p in pairs:
                    ins = nc.tensor.matmul(bank(7)[p % 2 * C:(p % 2 + 1) * C, 0:HW], cst["wfin"][:, p * C:(p + 1) * C],
                                           vals[i][:, p * HW:(p + 1) * HW], start=(p < 2), stop=(p >= PAIRS - 2),
                                           skip_group_check=True)
                if pairs[-1] == PAIRS - 1:
                    ins.then_inc(s_fin, 1)

            def windows(g, it, src, first_row):
                if g >= 4:
                    if g % 2 == 0:
                        pe.wait_ge(s_xTa, it * 6 + (g - 4) // 2 + 1)
                    else:
                        pe.wait_ge(s_xTd, it * 6 + (g - 5) // 2 + 1)
                for k in range(4):
                    j, w = divmod(4 * g + k, WINS)
                    row = first_row + w // 3 * STRIP + w % 3
                    ins = nc.tensor.transpose(bank(g % 4)[:, k * P:(k + 1) * P],
                                              images(src)[:, j, row * W:(row + WROWS) * W], ident)
                ins.then_inc(s_tr, 1)

            def convolve(n, k):
                h, j = CONV[n] // 2, CONV[n] % 2 * 2
                ky, single = divmod(k, 2)
                if k == 0:
                    if h == 0:
                        pe.wait_ge(s_dup0, CONV[n] + 1)
                    else:
                        pe.wait_ge(s_dup1, 2)
                    if n >= 2:
                        pe.wait_ge(s_omraw, n - 1)
                ins = nc.tensor.matmul(bank(4 + n % 2 * 2)[0:OM], womt[:, k * OM:(k + 1) * OM],
                                       shifted(dup[h], 3 * ky + 2 * single)[:, j:j + 2], start=(k == 0),
                                       stop=(k == TAPSTEPS - 1))
                if k == TAPSTEPS - 1:
                    ins.then_inc(s_conv, 1)

            def spread_mask(n):
                c, p = CONV[n // PAIRS], n % PAIRS
                if n == LAST:
                    pe.wait_ge(s_absx, ONE + PAIRS)
                    pe.wait_ge(s_absy, ONE + PAIRS)
                before = n - 4 if n < LAST else n - 3
                if before >= (0 if n < LAST else LAST):
                    taken(pe, before)
                if n < DIRECT:
                    if p == 0:
                        pe.wait_ge(s_mstack[n // PAIRS], 16 * 3)
                    nc.tensor.matmul(slice_bank(n), sel["selm"][:, p * P:(p + 1) * P],
                                     stack["m"][:, c * BANK:(c + 1) * BANK], start=True, stop=True).then_inc(s_mb, 1)
                    return
                if p == 0:
                    pe.wait_ge(s_parts, n // PAIRS + 1)
                for i in range(3):
                    ins = nc.tensor.matmul(slice_bank(n), sel["selpart"][0:OM, p * P:(p + 1) * P],
                                           parts[:, n // PAIRS % 2, i], start=(i == 0), stop=(i == 2))
                ins.then_inc(s_mb, 1)

            pe.wait_ge(s_wom, 16)
            for k in range(TAPSTEPS):
                convolve(0, k)
            pe.wait_ge(s_tall, J)
            for k in range(TAPSTEPS):
                convolve(1, k)
                windows(2 * k, 0, tall, WROWS * CENTER)
                windows(2 * k + 1, 0, tall, WROWS * CENTER)
            pe.wait_ge(s_xTa, 6)
            pe.wait_ge(s_xTd, 6)
            pe.wait_ge(s_rows, 16 * 3)
            pe.wait_ge(s_sel, 16 * len(SELS))
            pe.wait_ge(s_stack[0], 16 * 6)
            hat = 0
            for n in (2, 3):
                for k in range(TAPSTEPS):
                    convolve(n, k)
                    if k < PAIRS:
                        if k in HATS[n]:
                            select(hat, 0, hat + 1, 0)
                            hat += 1
                        spread_mask((n - 2) * PAIRS + k)
            for n in range(2 * PAIRS, LAST):
                spread_mask(n)
            taken(pe, LAST - 1)
            for g in range(AHEAD_X):
                issue_x(g, g, 1, max(g - 1, 0))
            for g in range(AHEAD):
                issue_y(g, g, 1, 0)
            pe.wait_ge(s_amax, 1)
            nc.tensor.matmul(bank(6)[0:1, 0:OM], amax[:, len(CONV):], ident[0:OM, 0:OM], start=True, stop=True).then_inc(s_amaxT, 1)
            for n in range(LAST, SLICES):
                spread_mask(n)
            pe.wait_ge(s_choice, 1)
            passes = pe.value_load(choice[0:1, 0:1], min_val=1, max_val=SHIFTS)
            taken(pe, SLICES - 1)
            for n in range(1, len(CONV)):
                pe.wait_ge(s_stack[n], 16 * 6)

            with pe.Fori(0, passes) as it:
                with pe.If(it > 0):
                    pe.wait_ge(s_staged, it)
                    pe.wait_ge(s_smp, ONE + it * UP)
                    pe.wait_ge(s_hx, ONE + it * UPX)
                    for g in range(12):
                        windows(g, it, staged, 0)
                    pe.wait_ge(s_xTa, (it + 1) * 6)
                    pe.wait_ge(s_xTd, (it + 1) * 6)
                    for p in range(PAIRS):
                        select(p, 0, it * HP + p + 1, it * (B + 1))
                        if p == 0:
                            for g in range(AHEAD_X):
                                issue_x(g, g, it * HP + 1, it * UPX + max(g - 1, 0))
                    for g in range(AHEAD):
                        issue_y(g, g, it * HP + 1, it * UP)
                with pe.Fori(0, J) as j:
                    for h in range(HALVES):
                        pe.wait_ge(s_xs, it * (B + 1) + j * 2 + (h + 1))
                        for u in range(UNITS):
                            g = h * UNITS + u
                            nxt, unit = divmod(u + AHEAD_X, UNITS)
                            issue_x(g + AHEAD_X, unit, it * HP + j * (2 * PAIRS) + ((h + nxt) * PAIRS + unit // DG + 1),
                                    it * UPX + j * (2 * UNITS) + (g + AHEAD_X - 1))
                            counts = (it * UP + j * (2 * UNITS) + (g + 1), it * (PAIRS * B) + j * (2 * PAIRS) + (h * PAIRS + u // DG))
                            nxt, unit = divmod(u + AHEAD, UNITS)
                            issue_y(g + AHEAD, unit, it * HP + j * (2 * PAIRS) + ((h + nxt) * PAIRS + unit // DG + 1),
                                    it * UP + j * (2 * UNITS) + (g + AHEAD - 1))
                            if u in (2, 3):
                                final(1 - h, [(0, 1), (2, 3, 4)][u - 2], it * (B + 1) + j * 2 + (h + 1),
                                      it * (PAIRS * B) + j * (2 * PAIRS) + (h * PAIRS + 1),
                                      it * HP + j * (2 * PAIRS) + (h + 1) * PAIRS)
                            if u % 4 == 2:
                                select_x(u // 4, j + (J if h == 0 else 1),
                                         it * HP + j * (2 * PAIRS) + ((h + 1) * PAIRS + u // 4 + 1))
                            if u in SELECT_Y:
                                p = SELECT_Y[u]
                                select_y(p, j + (J if h == 0 else 1), it * HP + j * (2 * PAIRS) + ((h + 1) * PAIRS + p + 1),
                                         it * (B + 1) + j * 2 + (h + 1))
                            if u % 2:
                                products(h, u - 1, (0, 1, 2, 3), *counts)
                final(1, range(PAIRS), it * (B + 1) + (B + 1), it * (PAIRS * B) + (PAIRS * B + 1), (it + 1) * HP)
            pe.wait_ge(s_acc, ONE + passes * (B + 1))
            pe.wait_ge(s_hx, ONE + passes * UPX)
            for c in range(OUTS - 1):
                nc.tensor.matmul(bank(c)[0:C], cst["fold"], acc[:, HW + c * BANK:][:, 0:BANK], start=True,
                                 stop=True).then_inc(s_fold, 1)


def _layout(a):
    import numpy as np

    def diag(w):
        o = np.zeros((HALVES * w.shape[0], HALVES * w.shape[1]), np.float32)
        for h in range(HALVES):
            o[h * w.shape[0]:(h + 1) * w.shape[0], h * w.shape[1]:(h + 1) * w.shape[1]] = w
        return np.pad(o, ((0, P - o.shape[0]), (0, P - o.shape[1])))

    def rows(v):
        v = np.concatenate([v] * HALVES)
        return np.pad(v, (0, P - v.shape[0]))

    i = np.arange(P)
    gnp = np.where(i[:, None] // GC == i[None] // GC, 1.0 / GC, 0.0)
    wq = a["L0_conv_W_qkv"].reshape(C, 4, C)
    headsum = np.zeros((P, 2, 2, HALVES * HEADS))
    spread = np.zeros((J, 2, HALVES * HEADS, J, 2, P))
    for p in range(P):
        for part in range(2):
            headsum[p, part, part, p // HD] = 1
            for j in range(J):
                spread[j, part, p // HD, j, part, p] = 1
    wd = a["L1_conv_w_dcn"].reshape(C, DG, CG, TAPS)
    wfin = np.zeros((DG, 2, CG, PAIRS, C), np.float32)
    for t in range(TAPS):
        wfin[:, t % 2, :, t // 2, :] = wd[:, :, :, t].transpose(1, 2, 0)
    order = [2 * ND + n for n in range(ND)] + [2 * n for n in range(ND)] + [2 * n + 1 for n in range(ND)]
    wo = a["L1_conv_w_om"][order].reshape(OM, C, TAPS).transpose(1, 2, 0)
    wom = np.zeros((2, C, 3, 2, OM), np.float32)
    for ky in range(3):
        wom[0, :, ky, 0], wom[1, :, ky, 0], wom[0, :, ky, 1] = (wo[:, 3 * ky + kx] for kx in range(3))
    bq = a["L0_conv_b_qkv"].reshape(C, 4)
    bias = np.stack([rows(bq[:, t]) for t in range(4)] + [
        rows(a["L0_conv_b1"]), rows(a["L0_conv_b2"]), rows(a["L0_conv_bp"]),
        np.pad(a["L1_conv_b_om"][order], (0, P - OM))], axis=1)
    table = np.tile([-float(WROWS) * (s - CENTER) for s in (2, 0, 1, 3, 4)], (P, 1))
    cf = np.concatenate([gnp, np.eye(P) - gnp, np.eye(P), wfin.reshape(P, -1), np.concatenate([np.eye(C)] * 2), bias, table] + [
        diag(wq[:, t].T) for t in range(4)] + [diag(a["L0_conv_W1"].T), diag(a["L0_conv_W2"].T),
                                               diag(a["L0_conv_Wp"].T), headsum.reshape(P, -1)], axis=1).astype(np.float32)

    sely, selx, selm = (np.zeros((STACK + 2, n, P), np.float32) for n in (PAIRS, TAPS, PAIRS))
    for t in range(TAPS):
        p, ab = divmod(t, 2)
        for d in range(DG):
            src = [i * ND + d * TAPS + t for i in range(3)]
            for part in range(2):
                for r in range(WROWS):
                    c = part * 64 + ab * 32 + d * WROWS + r
                    sely[src, p, c] = 1
                    sely[STACK, p, c] = 1
                    sely[STACK + 1, p, c] = -r
                for x in range(W):
                    c = part * 64 + d * W + x
                    selx[src, t, c] = 1
                    selx[STACK, t, c] = 1
                    selx[STACK + 1, t, c] = t % 3 - 1 - x
            c = slice(d * 32 + ab * CG, d * 32 + ab * CG + CG)
            selm[src, p, c] = 0.5
            selm[STACK + 1, p, c] = 0.5
    selpart = np.zeros_like(selm)
    selpart[0:ND] = selm[0:ND]
    bx, by = np.zeros((P, DG, P)), np.zeros((P, DG, 2, P))
    for d in range(DG):
        for part in range(2):
            for m in range(P):
                bx[part * 64 + d * W + m % W, d, m] = 1 - 2 * part
                for ab in range(2):
                    by[part * 64 + ab * 32 + d * WROWS + m // W, d, ab, m] = 1 - 2 * part
    n = np.arange(ALL) % HW
    f16 = np.float16

    def bf16_bits(v):
        return (v.astype(np.float32).view(np.uint32) >> 16).astype(np.uint16)

    return {
        "x": a["x"].reshape(HALVES, J, C, HW).transpose(0, 2, 1, 3).reshape(P, N), "cf": cf,
        "wom": wom.reshape(P, -1),
        "bcast": np.concatenate([bx.reshape(P, -1), by.reshape(P, -1), spread.reshape(P, -1)], 1).astype(f16),
        "sely": bf16_bits(sely.reshape(STACK + 2, -1)), "selx": bf16_bits(selx.reshape(STACK + 2, -1)),
        "selm": bf16_bits(selm.reshape(STACK + 2, -1)), "selpart": bf16_bits(selpart.reshape(STACK + 2, -1)),
        "rowsy": bf16_bits(np.stack([n // W % STRIP + REACH, np.ones(ALL)])),
        "rowsx": bf16_bits(np.stack([n % W, np.ones(ALL)])),
    }


def kernel(**inputs):
    import numpy as np
    import concourse.bacc as bacc
    from concourse.bass_utils import run_bass_kernel_spmd as run

    arrays = {k: np.ascontiguousarray(v) for k, v in _layout({k: np.asarray(v) for k, v in inputs.items()}).items()}
    nc = bacc.Bacc("TRN2", target_bir_lowering=False, num_devices=1)
    d = {k: nc.dram_tensor("in_" + k, v.shape, mybir.dt.from_np(v.dtype), kind="ExternalInput").ap() for k, v in arrays.items()}
    out = nc.dram_tensor("out", (C, ALL), mybir.dt.float32, kind="ExternalOutput").ap()
    bass_local_attention_then_deformable_conv(
        nc, d["x"], d["cf"], d["wom"],
        {k: d[k] for k in ("bcast", "sely", "selx", "selm", "selpart")}, {"y": d["rowsy"], "x": d["rowsx"]}, out)
    r = run(nc, [{"in_" + k: v for k, v in arrays.items()}], core_ids=[0])
    y = r.results[0]["out"].reshape(C, J, HALVES, H, W)
    return np.ascontiguousarray(y.transpose(2, 1, 0, 3, 4)).reshape(B, C, H, W)
```
